# Optimizing a Trainium2 kernel written in Bass

```python
import numpy as np
import jax
import jax.numpy as jnp

def _softmax(x, axis=-1):
    return jax.nn.softmax(x, axis=axis)

def _gelu(x):
    return jax.nn.gelu(x, approximate=True)

def _silu(x):
    return jax.nn.silu(x)

def _sigmoid(x):
    return jax.nn.sigmoid(x)

def _layernorm(x, axis=-1, eps=1e-05):
    m = jnp.mean(x, axis=axis, keepdims=True)
    v = jnp.var(x, axis=axis, keepdims=True)
    return (x - m) / jnp.sqrt(v + eps)

def _scatter_add(tgt, idx, src, axis=0):
    return tgt.at[idx].add(src)

def _segment_sum(src, seg, n):
    return jax.ops.segment_sum(src, seg, n)
kernel_name = 'mk_sandwich_d1_jaxref_r8_9cdc19'

def setup_inputs(seed: int=0):
    np.random.seed(seed)
    _w = jnp.asarray

    def _L0_attn_setup():
        import jax, jax.numpy as jnp
        import numpy as np
        EPS = 1e-08

        def rms_norm(x, scale):
            d = x.shape[-1]
            norm = jnp.linalg.norm(x, ord=2, axis=-1, keepdims=True)
            rms = norm * d ** (-0.5)
            return scale * (x / (rms + EPS))
        key = jax.random.key(seed)
        ks = jax.random.split(key, 4)
        B, N, C, H = (2, 256, 128, 16)
        hd = C // H
        x = jax.random.normal(ks[0], (B, N, C), dtype=jnp.float32)
        Wqkv = jax.random.normal(ks[1], (C, 3 * C), dtype=jnp.float32) * C ** (-0.5)
        Wproj = jax.random.normal(ks[2], (C, C), dtype=jnp.float32) * C ** (-0.5)
        bproj = jnp.zeros((C,), dtype=jnp.float32)
        q_scale = jnp.ones((hd,), dtype=jnp.float32)
        k_scale = jnp.ones((hd,), dtype=jnp.float32)
        return {'x': x, 'Wqkv': Wqkv, 'Wproj': Wproj, 'bproj': bproj, 'q_scale': q_scale, 'k_scale': k_scale}
    _L0_attn_in = _L0_attn_setup()

    def _L0_ffn_setup():
        import jax, jax.numpy as jnp
        import numpy as np
        E, K = (8, 2)
        DM, DE = (128, 352)
        B, S = (1, 256)
        EPS = 1e-06

        def _rmsnorm(x, w):
            var = jnp.mean(jnp.square(x), axis=-1, keepdims=True)
            return x * jax.lax.rsqrt(var + EPS) * w
        key = jax.random.key(seed)
        kx, kg, k1, k2, k3 = jax.random.split(key, 5)

        def kaiming_uniform(k, shape, fan_in):
            bound = 1.0 / np.sqrt(fan_in)
            return jax.random.uniform(k, shape, jnp.float32, -bound, bound)
        return {'x': jax.random.normal(kx, (B, S, DM), jnp.float32), 'gate_w': kaiming_uniform(kg, (E, DM), DM), 'rms_w': jnp.ones((DM,), jnp.float32), 'W1': kaiming_uniform(k1, (E, DE, DM), DE * DM), 'W2': kaiming_uniform(k2, (E, DE, DM), DE * DM), 'W3': kaiming_uniform(k3, (E, DM, DE), DM * DE)}
    _L0_ffn_in = _L0_ffn_setup()
    _d = {'L0_attn_x': _L0_attn_in['x'], 'L0_attn_Wqkv': _L0_attn_in['Wqkv'], 'L0_attn_Wproj': _L0_attn_in['Wproj'], 'L0_attn_bproj': _L0_attn_in['bproj'], 'L0_attn_q_scale': _L0_attn_in['q_scale'], 'L0_attn_k_scale': _L0_attn_in['k_scale'], 'L0_ffn_gate_w': _L0_ffn_in['gate_w'], 'L0_ffn_rms_w': _L0_ffn_in['rms_w'], 'L0_ffn_W1': _L0_ffn_in['W1'], 'L0_ffn_W2': _L0_ffn_in['W2'], 'L0_ffn_W3': _L0_ffn_in['W3']}
    _x0 = _d['L0_attn_x']
    _d['L0_attn_x'] = jax.random.normal(jax.random.fold_in(jax.random.key(seed), 1), (4, 512, 128), dtype=_x0.dtype)
    del _x0
    return _d

def reference(L0_attn_x, L0_attn_Wqkv, L0_attn_Wproj, L0_attn_bproj, L0_attn_q_scale, L0_attn_k_scale, L0_ffn_gate_w, L0_ffn_rms_w, L0_ffn_W1, L0_ffn_W2, L0_ffn_W3):

    def _L0_attn_ref(x, Wqkv, Wproj, bproj, q_scale, k_scale):
        import jax, jax.numpy as jnp
        import numpy as np
        EPS = 1e-08

        def rms_norm(x, scale):
            d = x.shape[-1]
            norm = jnp.linalg.norm(x, ord=2, axis=-1, keepdims=True)
            rms = norm * d ** (-0.5)
            return scale * (x / (rms + EPS))
        B, N, C = x.shape
        H = 16
        hd = C // H
        scale = hd ** (-0.5)
        qkv = (x @ Wqkv).reshape(B, N, 3, H, hd)
        qkv = jnp.transpose(qkv, (2, 0, 3, 1, 4))
        q, k, v = (qkv[0], qkv[1], qkv[2])
        q = rms_norm(q, q_scale)
        k = rms_norm(k, k_scale)
        attn = jnp.einsum('bhnc,bhmc->bhnm', q, k) * scale
        attn = jax.nn.softmax(attn, axis=-1)
        out = jnp.einsum('bhnm,bhmc->bhnc', attn, v)
        out = jnp.transpose(out, (0, 2, 1, 3)).reshape(B, N, C)
        return out @ Wproj + bproj

    def _L0_ffn_ref(x, gate_w, rms_w, W1, W2, W3):
        import jax, jax.numpy as jnp
        import numpy as np
        E, K = (8, 2)
        DM, DE = (128, 352)
        B, S = (1, 256)
        EPS = 1e-06

        def _rmsnorm(x, w):
            var = jnp.mean(jnp.square(x), axis=-1, keepdims=True)
            return x * jax.lax.rsqrt(var + EPS) * w
        y = _rmsnorm(x, rms_w)
        logits = jnp.einsum('bsd,ed->bse', y, gate_w)
        vals, idx = jax.lax.top_k(logits, K)
        w = jax.nn.softmax(vals, axis=-1)
        w_full = jnp.einsum('bsk,bske->bse', w, jax.nn.one_hot(idx, E, dtype=x.dtype))
        up = jnp.einsum('bsd,end->bsen', y, W1)
        gate = jnp.einsum('bsd,end->bsen', y, W2)
        h = jax.nn.silu(up) * gate
        out = jnp.einsum('bsen,emn->bsem', h, W3)
        comb = jnp.einsum('bsem,bse->bsm', out, w_full)
        return x + comb
    x = L0_attn_x
    x = x + _layernorm(_L0_attn_ref(_layernorm(x, axis=-1), L0_attn_Wqkv, L0_attn_Wproj, L0_attn_bproj, L0_attn_q_scale, L0_attn_k_scale), axis=-1)
    x = x + _layernorm(_L0_ffn_ref(_layernorm(x, axis=-1), L0_ffn_gate_w, L0_ffn_rms_w, L0_ffn_W1, L0_ffn_W2, L0_ffn_W3), axis=-1)
    return x

_drawn_inputs = setup_inputs


def setup_inputs(seed=0):
    import zlib

    import numpy as np

    out = dict(_drawn_inputs(seed))
    spreads = {'L0_attn_bproj': (0.0, 0.1),
     'L0_attn_q_scale': (1.0, 0.2),
     'L0_attn_k_scale': (1.0, 0.2),
     'L0_ffn_rms_w': (1.0, 0.6)}
    factors = {'L0_ffn_gate_w': 47.621, 'L0_ffn_W1': 44.297, 'L0_ffn_W2': 43.579, 'L0_ffn_W3': 43.438}
    for name, (base, spread) in spreads.items():
        noise = np.random.default_rng([zlib.crc32(name.encode()), seed]).standard_normal(out[name].shape)
        drawn = base * np.exp(spread * noise) if base else spread * noise
        out[name] = jnp.asarray(drawn.astype(out[name].dtype))
    for name, factor in factors.items():
        out[name] = (out[name] * factor).astype(out[name].dtype)
    return out
```

```python
import concourse.bass as bass
from concourse import mybir
from contextlib import ExitStack

F32 = mybir.dt.float32
F16 = mybir.dt.float16
U32 = mybir.dt.uint32
ALU = mybir.AluOpType
ACT = mybir.ActivationFunctionType
AX = mybir.AxisListType

P = 128
B, N, C = 4, 512, 128
T = N // P
H, HD = 16, 8
G = H // 4
E, DE = 8, 352
PARTS = [(0, 128), (128, 128), (256, 96)]
TILES = E * len(PARTS)
UNITS = G * T
SLOTS = TILES
SAFE = 80.0
LN_EPS, QK_EPS, FFN_EPS = 1e-5, 1e-8, 1e-6

MISC = {2: ["xT"], 3: ["qkv0"], 4: ["qkv1"], 5: ["oT0", "qkv2"], 6: ["qkv3"], 9: ["oT1"], 13: ["oT2"],
        16: ["stack0"], 17: ["oT3", "stack1"], 18: ["aT", "stack2"], 19: ["proj", "stack3"],
        22: ["yT"], 23: ["logits"]}
PREP_USES = ["xT", "qkv0", "qkv1", "qkv2", "qkv3", "stack0", "stack1", "stack2", "stack3"]
ALL_USES = [name for slot in sorted(MISC) for name in MISC[slot]]
POST_USES = [name for name in ALL_USES if name not in PREP_USES]
N_PREP, N_ALL = len(PREP_USES), len(ALL_USES)


def spread(ap, axis, n):
    shape = list(ap.shape)
    shape[axis] = n
    return ap.broadcast_to(shape)


class Uses:

    def __init__(self, b, prep):
        self.base = 0 if b is None else b * N_ALL + N_PREP
        self.names = PREP_USES if b is None else ALL_USES if prep else POST_USES

    def __getitem__(self, name):
        return self.base + self.names.index(name)


class Steps:

    def __init__(self, eng, sem, b, per):
        self.eng, self.sem, self.b, self.per, self.n = eng, sem, b, per, 0

    def do(self, instruction):
        self.n += 1
        assert self.n <= self.per
        instruction.then_inc(self.sem, 1)

    def wait(self):
        self.eng.wait_ge(self.sem, self.b * self.per + self.n)


def layers(nc, x, wqkv, wproj, bproj, q_scale, k_scale, gate_wT, rms_w, w1T, w2T, w3T, out):
    with ExitStack() as ctx:
        def sb(name, shape, dt=F32):
            return ctx.enter_context(nc.sbuf_tensor(name, shape, dt))

        def sem(name):
            return ctx.enter_context(nc.semaphore(name))

        stream = sb("stream", [P, B * T, C])
        wqkv_sb = sb("wqkv_sb", [P, 3 * C])
        wproj_sb = sb("wproj_sb", [P, C])
        bproj_sb = sb("bproj_sb", [P, C])
        rms_sb = sb("rms_sb", [P, C])
        qs_sb = sb("qs_sb", [P, H * HD])
        ks_sb = sb("ks_sb", [P, H * HD])
        qks = sb("qks", [P, H * HD])
        w_raw = sb("w_raw", [P, 2, E * DE])
        w_hi = sb("w_hi", [P, 2, E * DE], F16)
        w_lo = sb("w_lo", [P, 2, E * DE], F16)
        w3 = sb("w3", [P, E, 3, C])
        gw = sb("gw", [P, E])
        gw_hi = sb("gw_hi", [P, E], F16)
        gw_lo = sb("gw_lo", [P, E], F16)
        ident = sb("ident", [P, P])
        ident16 = sb("ident16", [P, P], F16)
        expert_no = sb("expert_no", [P, E])
        half = sb("half", [P, T * 2 * H])
        neg_half = sb("neg_half", [P, T])
        qks_neg = sb("qks_neg", [P, H * HD])
        qks_max = sb("qks_max", [P, 1])
        shift0 = sb("shift0", [P, 1])
        shift = sb("shift", [P, 1])
        held_dve = sb("held_dve", [P, 1])
        held_pool = sb("held_pool", [P, 1])

        stats = sb("stats", [P, T, 6])
        moments = sb("moments", [P, T, 2])
        var_eps = sb("var_eps", [P, T])
        rstd = sb("rstd", [P, T])
        xn = sb("xn", [P, T, C])
        xnT = sb("xnT", [P, N])
        qkv = sb("qkv", [P, T, 3 * C])
        squares = sb("squares", [P, T, 2 * C])
        ssq = sb("ssq", [P, T * 2 * H])
        msq = sb("msq", [P, T * 2 * H])
        rms = sb("rms", [P, T * 2 * H])
        rms_eps = sb("rms_eps", [P, T * 2 * H])
        inv = sb("inv", [P, T * 2 * H])
        qn = sb("qn", [P, T * H, HD])
        kn = sb("kn", [P, T, H * HD])
        kw = sb("kw", [P, T * H, HD])
        stack = sb("stack", [P, 2, T * H, 2, 2, HD], F16)
        qkT = sb("qkT", [P, 2 * G, N], F16)
        v_ext = sb("v_ext", [P, T * H, 32])

        PR = 8
        probs = sb("probs", [P, PR, N])
        oT = sb("oT", [P, N])
        recip = sb("recip", [P, T, 4])
        attn = sb("attn", [P, T, C])
        attnT = sb("attnT", [P, N])
        z = sb("z", [P, T, C])
        zn = sb("zn", [P, T, C])
        p_stats = sb("p_stats", [P, T, 6])
        p_moments = sb("p_moments", [P, T, 2])
        p_var = sb("p_var", [P, T])
        p_rstd = sb("p_rstd", [P, T])
        x1 = sb("x1", [P, T, C])
        xin = sb("xin", [P, T, C])
        xin_sq = sb("xin_sq", [P, T, C])
        y = sb("y", [P, T, C])
        y_split = sb("y_split", [P, 2, T, C], F16)
        yT = sb("yT", [P, B, 2 * N], F16)
        logit = sb("logit", [P, T, E])
        top = sb("top", [P, T, E])
        top_at = sb("top_at", [P, T, E], U32)
        top_no = sb("top_no", [P, T, 2])
        gap = sb("gap", [P, T])
        e2 = sb("e2", [P, T])
        e_sum = sb("e_sum", [P, T])
        e_inv = sb("e_inv", [P, T])
        w_top = sb("w_top", [P, 2, T])
        w_a = sb("w_a", [P, T, E])
        w_b = sb("w_b", [P, T, E])
        route = sb("route", [P, B, T * E])

        route_now = sb("route_now", [P, T * E])
        th = sb("th", [P, 2, N])
        act2 = sb("act2", [P, 2, N])
        HR = 3
        hid = sb("hid", [P, HR, N])
        acc = sb("acc", [P, T, C])
        f_stats = sb("f_stats", [P, T, 6])
        f_moments = sb("f_moments", [P, T, 2])
        f_var = sb("f_var", [P, T])
        f_rstd = sb("f_rstd", [P, T])
        fn = sb("fn", [P, T, C])
        result = sb("result", [P, T, C])

        bank = [ctx.enter_context(nc.psum_tensor(f"bank{i}", [P, N], F32)) for i in range(8)]
        SR = 3
        score = bank[0:SR]
        o_bank, up, gate, down, misc = bank[3:8]
        misc16 = misc[:, :].bitcast(F16)

        s_x0, s_x, s_small, s_attn_w, s_ffn_w, s_w3 = (
            sem(n) for n in ("x0_in", "x_in", "small_in", "attn_w_in", "ffn_w_in", "w3_in"))
        s_id0, s_ident, s_ident16, s_const, s_vzero = (
            sem(n) for n in ("ident_zero", "ident", "ident16", "constants", "v_zero"))
        s_c = sem("constant_steps")
        s_split = sem("weights_split")
        s_full, s_free = sem("misc_full"), sem("misc_free")
        s_prep = sem("prep_steps")
        s_var, s_rstd = sem("prep_var"), sem("prep_rstd")
        s_xn, s_msq, s_rms = sem("xn_ready"), sem("msq_ready"), sem("rms_ready")
        s_stack, s_v = sem("stack_ready"), sem("v_ready")
        s_qk, s_exp, s_pv, s_o, s_attn = (
            sem(n) for n in ("scores_done", "probs_done", "pv_done", "o_copied", "attn_steps"))
        s_post, s_pvar, s_prstd, s_y = (
            sem(n) for n in ("post_steps", "post_var", "post_rstd", "y_ready"))
        s_gap, s_e2 = sem("gap_ready"), sem("e2_ready")
        s_up, s_gate, s_tanh, s_act, s_hid, s_dn, s_comb = (
            sem(n) for n in ("up_done", "gate_done", "tanh_done", "act_done", "hid_done", "down_done", "combined"))
        s_route_now = sem("route_now")
        s_fin, s_fvar, s_frstd, s_result, s_out = (
            sem(n) for n in ("final_steps", "final_var", "final_rstd", "result_ready", "out_written"))

        block = ctx.enter_context(nc.Block())

        def tile_of(ap, b, t):
            if isinstance(b, int):
                return ap[:, b * T + t, :]
            return ap[:, bass.ds(b * T + t, 1), :].rearrange("p a c -> p (a c)")

        def batch_of(ap, b):
            if isinstance(b, int):
                return ap[:, b, :]
            return ap[:, bass.ds(b, 1), :].rearrange("p a n -> p (a n)")

        def some(b):
            return not isinstance(b, int) or b > 0

        def iterations(eng, run):
            run(None, None, 0)
            run(0, None, 1)
            with eng.Fori(1, B - 1) as b:
                run(b, b - 1, b + 1)
            run(B - 1, B - 2, None)
            run(None, B - 1, None)

        @block.sync
        def _(sp):
            rows = x.rearrange("b (t p) c -> p (b t) c", p=P)
            sp.dma_start(stream[:, 0:T, :], rows[:, 0:T, :]).then_inc(s_x0, 16)
            sp.dma_start(wqkv_sb[:, :], wqkv).then_inc(s_attn_w, 16)
            sp.dma_start(qs_sb[:, :], q_scale).then_inc(s_small, 16)
            sp.dma_start(ks_sb[:, :], k_scale).then_inc(s_small, 16)
            sp.dma_start(stream[:, T:B * T, :], rows[:, T:B * T, :]).then_inc(s_x, 16)
            sp.dma_start(wproj_sb[:, :], wproj).then_inc(s_attn_w, 16)
            sp.dma_start(bproj_sb[:, :], bproj).then_inc(s_attn_w, 16)
            sp.dma_start(rms_sb[:, :], rms_w).then_inc(s_attn_w, 16)
            sp.dma_start(gw[:, :], gate_wT).then_inc(s_ffn_w, 16)
            sp.dma_start(w_raw[:, 0, :], w1T).then_inc(s_ffn_w, 16)
            sp.dma_start(w_raw[:, 1, :], w2T).then_inc(s_ffn_w, 16)
            for i, (first, rows_i) in enumerate(PARTS):
                sp.dma_start(w3[0:rows_i, :, i, :],
                             w3T[:, first:first + rows_i, :].rearrange("e p m -> p e m")).then_inc(s_w3, 16)

            def store(b):
                sp.wait_ge(s_result, b + 1)
                dst = out[b] if isinstance(b, int) else out[bass.ds(b, 1)].rearrange("a n c -> (a n) c")
                sp.dma_start(dst.rearrange("(t p) c -> p t c", p=P), result[:, :, :]).then_inc(s_out, 16)

            def run(att, ffn, prep):
                if ffn is not None:
                    store(ffn)

            iterations(sp, run)
            sp.wait_ge(s_out, 16 * B)

        @block.gpsimd
        def _(pool):
            pool.memset(ident[:, :], 0.0).then_inc(s_id0, 1)
            pool.memset(neg_half[:, :], -0.5).then_inc(s_const, 1)
            pool.memset(half[:, :], 0.5).then_inc(s_const, 1)
            pool.wait_ge(s_id0, 1)
            pool.affine_select(out=ident[:, :], in_=ident[:, :], compare_op=ALU.not_equal, fill=1.0,
                               base=0, pattern=[[-1, P]], channel_multiplier=1).then_inc(s_ident, 1)
            pool.iota(expert_no[:, :], [[1, E]], base=0, channel_multiplier=0,
                      allow_small_or_imprecise_dtypes=True).then_inc(s_const, 1)
            pool.memset(v_ext[:, :, :], 0.0).then_inc(s_vzero, 1)
            pool.wait_ge(s_vzero, 1)
            pool.memset(v_ext[:, :, HD:HD + 1], 1.0).then_inc(s_vzero, 1)
            pool.wait_ge(s_vzero, 2)
            pool.wait_ge(s_const, 3)

            def norm_power(b, ready, done, src, dst, n, of):
                pool.wait_ge(ready, b * of + n + 1)
                pool.tensor_tensor(dst[:, :], src[:, :], neg_half[:, :], ALU.pow).then_inc(done, 1)

            def run(att, ffn, prep):
                if prep is not None:
                    norm_power(prep, s_var, s_rstd, var_eps, rstd, 0, 1)
                    pool.wait_ge(s_msq, prep + 1)
                    pool.tensor_tensor(rms[:, :], msq[:, :], half[:, :], ALU.pow).then_inc(s_rms, 1)
                    if some(prep):
                        pool.wait_ge(s_pv, prep * UNITS)
                    pool.wait_ge(s_free, Uses(att, True)["qkv3"] + 1)
                    pool.tensor_tensor(held_pool[:, :], half[:, 0:1], half[:, 0:1], ALU.mult)
                    for t in range(T):
                        ins = pool.tensor_copy(v_ext[:, t * H:(t + 1) * H, 0:HD],
                                               qkv[:, t, 2 * C:3 * C].rearrange("p (h c) -> p h c", c=HD))
                    ins.then_inc(s_v, 1)
                if att is not None:
                    for n in range(3):
                        norm_power(att, s_pvar, s_prstd, p_var, p_rstd, n, 3)
                if ffn is not None:
                    norm_power(ffn, s_fvar, s_frstd, f_var, f_rstd, 0, 1)

            iterations(pool, run)

        @block.tensor
        def _(pe):
            pe.wait_ge(s_ident, 1)
            pe.wait_ge(s_attn_w, 64)
            pe.wait_ge(s_ident16, 1)

            def fill(uses, name):
                n = uses[name]
                if not isinstance(n, int) or n > 0:
                    pe.wait_ge(s_free, n)

            def transposes(dst, src, what):
                for t in range(T):
                    ins = pe.transpose(dst[:, t * P:(t + 1) * P], src(t), what[:, :])
                return ins

            def misc_use(name, uses, att, prep):
                if name == "xT":
                    pe.wait_ge(s_xn, prep + 1)
                    fill(uses, name)
                    ins = transposes(misc, lambda t: xn[:, t, :], ident)
                elif name.startswith("qkv"):
                    t = int(name[3:])
                    fill(uses, name)
                    ins = pe.matmul(misc[:, 0:3 * C], xnT[:, t * P:(t + 1) * P], wqkv_sb[:, :],
                                    start=True, stop=True)
                elif name.startswith("stack"):
                    t = int(name[5:])
                    pe.wait_ge(s_stack, prep + 1)
                    fill(uses, name)
                    for qk in range(2):
                        for g in range(G):
                            at = (qk * G + g) * P
                            src = stack[:, qk, t * H + 4 * g:t * H + 4 * g + 4, :, :, :]
                            ins = pe.transpose(misc16[:, at:at + P],
                                               src.rearrange("p h a b c -> p (h a b c)"), ident16[:, :])
                elif name.startswith("oT"):
                    g = int(name[2:])
                    pe.wait_ge(s_o, att * G + g + 1)
                    fill(uses, name)
                    ins = transposes(misc, lambda t: oT[:, t * P:(t + 1) * P], ident)
                elif name == "aT":
                    fill(uses, name)
                    pe.wait_ge(s_free, uses["oT3"] + 1)
                    ins = transposes(misc, lambda t: attn[:, t, :], ident)
                elif name == "proj":
                    fill(uses, name)
                    pe.wait_ge(s_free, uses["aT"] + 1)
                    for t in range(T):
                        ins = pe.matmul(misc[:, t * C:(t + 1) * C], attnT[:, t * P:(t + 1) * P],
                                        wproj_sb[:, :], start=True, stop=True)
                elif name == "yT":
                    pe.wait_ge(s_y, att + 1)
                    fill(uses, name)
                    for s in range(2):
                        for t in range(T):
                            at = s * N + t * P
                            ins = pe.transpose(misc16[:, at:at + P], y_split[:, s, t, :], ident16[:, :])
                elif name == "logits":
                    fill(uses, name)
                    now = batch_of(yT, att)
                    for t in range(T):
                        for i, (s, w) in enumerate(((0, gw_hi), (0, gw_lo), (1, gw_hi), (1, gw_lo))):
                            at = s * N + t * P
                            ins = pe.matmul(misc[:, t * E:(t + 1) * E], yT_static(at), w[:, :],
                                            start=i == 0, stop=i == 3)
                ins.then_inc(s_full, 1)

            def yT_static(at):
                return y_now[:, at:at + P]

            def scores(b, u, pair):
                g, m = divmod(u, T)
                for j in (2 * pair, 2 * pair + 1):
                    n = 4 * u + j
                    if n >= SR:
                        pe.wait_ge(s_exp, b * 4 * UNITS + n - SR + 1)
                    elif some(b):
                        pe.wait_ge(s_exp, b * 4 * UNITS)
                    r = slice(32 * j, 32 * j + 32)
                    pe.matmul(score[n % SR][:, :], qkT[r, G + g, m * P:(m + 1) * P], qkT[r, g, :],
                              start=True, stop=True).then_inc(s_qk, 1)

            def weighted(b, u):
                g, m = divmod(u, T)
                pe.wait_ge(s_exp, b * 4 * UNITS + 4 * u + 4)
                if u == 0:
                    pe.wait_ge(s_v, b + 1)
                if m == 0 and (g > 0 or some(b)):
                    pe.wait_ge(s_o, b * G + g)
                for j in range(4):
                    ins = pe.matmul(o_bank[32 * j:32 * j + 32, :], v_ext[:, m * H + 4 * g + j, :],
                                    probs[:, (4 * u + j) % PR, :], start=m == 0, stop=m == T - 1,
                                    skip_group_check=True)
                ins.then_inc(s_pv, 1)

            def expand(b, k, which, y_b):
                e, i = divmod(k, len(PARTS))
                at, rows = e * DE + PARTS[i][0], PARTS[i][1]
                dst, done, used = ((up, s_up, s_act), (gate, s_gate, s_hid))[which]
                if k > 0 or some(b):
                    pe.wait_ge(used, b * TILES + k)
                hi, lo = (w[:, which, at:at + rows] for w in (w_hi, w_lo))
                pe.matmul(dst[0:rows, :], hi, y_b[:, 0:N], start=True, stop=False)
                pe.matmul(dst[0:rows, :], hi, y_b[:, N:2 * N], start=False, stop=False)
                pe.matmul(dst[0:rows, :], lo, y_b[:, 0:N], start=False, stop=True).then_inc(done, 1)

            def contract(b, k):
                e, i = divmod(k, len(PARTS))
                rows = PARTS[i][1]
                pe.wait_ge(s_hid, b * TILES + k + 1)
                if i == 0 and (e > 0 or some(b)):
                    pe.wait_ge(s_comb, b * E + e)
                for t in range(T):
                    ins = pe.matmul(down[:, t * C:(t + 1) * C], hid[0:rows, k % HR, t * P:(t + 1) * P],
                                    w3[0:rows, e, i, :], start=i == 0 and t == 0,
                                    stop=i == len(PARTS) - 1, skip_group_check=True)
                ins.then_inc(s_dn, 1)

            def run(att, ffn, prep):
                nonlocal y_now
                if att is None and ffn is None:
                    uses = Uses(None, True)
                    for name in PREP_USES:
                        misc_use(name, uses, None, prep)
                    return
                uses = Uses(att, prep is not None) if att is not None else None
                if att is not None:
                    before = Uses(att - 1, True) if some(att) else Uses(None, True)
                    pe.wait_ge(s_free, before["stack3"] + 1)
                    y_now = batch_of(yT, att)
                if ffn is not None:
                    y_ffn = batch_of(yT, ffn)
                    if att is None:
                        pe.wait_ge(s_free, Uses(ffn, False)["yT"] + 1)
                for s in range(SLOTS):
                    if att is not None and s < UNITS:
                        scores(att, s, 0)
                    if ffn is not None:
                        expand(ffn, s, 0, y_ffn)
                        expand(ffn, s, 1, y_ffn)
                    if att is not None and s < UNITS:
                        scores(att, s, 1)
                    if att is not None and 1 <= s <= UNITS:
                        weighted(att, s - 1)
                    if ffn is not None and s >= 1:
                        contract(ffn, s - 1)
                    if att is not None:
                        if ffn is None and s == UNITS + 1:
                            pe.wait_ge(s_split, 4)
                            pe.wait_ge(s_w3, 48)
                        for name in MISC.get(s, ()):
                            if name in uses.names:
                                misc_use(name, uses, att, prep)
                if ffn is not None:
                    contract(ffn, SLOTS - 1)

            y_now = None
            iterations(pe, run)

        @block.scalar
        def _(act):
            act.wait_ge(s_c, 6)

            def copy_out(uses, name, dst, src):
                act.wait_ge(s_full, uses[name] + 1)
                act.activation(dst, src, ACT.Copy).then_inc(s_free, 1)

            def misc_use(name, uses, att, prep):
                if name == "xT":
                    copy_out(uses, name, xnT[:, :], misc[:, :])
                elif name.startswith("qkv"):
                    if name == "qkv0" and some(prep):
                        act.wait_ge(s_v, prep)
                    t = int(name[3:])
                    copy_out(uses, name, qkv[:, t, :], misc[:, 0:3 * C])
                elif name.startswith("stack"):
                    t = int(name[5:])
                    copy_out(uses, name, qkT[:, :, t * P:(t + 1) * P],
                             misc16.rearrange("p (a n) -> p a n", n=P))
                elif name == "aT":
                    copy_out(uses, name, attnT[:, :], misc[:, :])
                elif name == "yT":
                    copy_out(uses, name, batch_of(yT, att), misc16)

            def exps(b, u, pair):
                for j in (2 * pair, 2 * pair + 1):
                    n = 4 * u + j
                    act.wait_ge(s_qk, b * 4 * UNITS + n + 1)
                    if u >= 2:
                        act.wait_ge(s_pv, b * UNITS + u - 1)
                    elif some(b):
                        act.wait_ge(s_pv, b * UNITS)
                    act.activation(probs[:, n % PR, :], score[n % SR][:, :], ACT.Exp,
                                   bias=shift[:, :]).then_inc(s_exp, 1)

            def tanh(b, k):
                rows = PARTS[k % len(PARTS)][1]
                act.wait_ge(s_up, b * TILES + k + 1)
                if k >= 2:
                    act.wait_ge(s_act, b * TILES + k - 1)
                elif some(b):
                    act.wait_ge(s_act, b * TILES)
                act.activation(th[0:rows, k % 2, :], up[0:rows, :], ACT.Tanh, scale=0.5).then_inc(s_tanh, 1)

            def run(att, ffn, prep):
                if att is None and ffn is None:
                    for name in PREP_USES:
                        misc_use(name, Uses(None, True), None, prep)
                    return
                uses = Uses(att, prep is not None) if att is not None else None
                for s in range(SLOTS):
                    if att is not None and s < UNITS:
                        exps(att, s, 0)
                    if ffn is not None:
                        tanh(ffn, s)
                    if att is not None and s < UNITS:
                        exps(att, s, 1)
                    if att is not None:
                        for name in MISC.get(s, ()):
                            if name in uses.names:
                                misc_use(name, uses, att, prep)
                        if s == SLOTS - 1:
                            act.wait_ge(s_gap, att + 1)
                            act.activation(e2[:, :], gap[:, :], ACT.Exp).then_inc(s_e2, 1)

            iterations(act, run)

        @block.vector
        def _(dve):
            v = dve
            c = Steps(dve, s_c, 0, 100)
            dve.wait_ge(s_small, 32)
            c.do(v.scalar_tensor_tensor(out=qks[:, :], in0=qs_sb[:, :], scalar=HD ** -0.5, in1=ks_sb[:, :],
                                        op0=ALU.mult, op1=ALU.mult))
            c.wait()
            c.do(v.tensor_scalar(qks_neg[:, :], qks[:, :], -1.0, None, ALU.mult))
            c.wait()
            c.do(v.tensor_tensor(squares[:, 0, 0:P], qks[:, :], qks_neg[:, :], ALU.max))
            c.wait()
            c.do(v.reduce_max(qks_max[:, :], squares[:, 0, 0:P], AX.X))
            c.wait()
            c.do(v.tensor_scalar(shift0[:, :], qks_max[:, :], -float(HD), SAFE, ALU.mult, ALU.add))
            c.wait()
            c.do(v.tensor_scalar(shift[:, :], shift0[:, :], 0.0, None, ALU.min))
            dve.wait_ge(s_ident, 1)
            v.tensor_copy(ident16[:, :], ident[:, :]).then_inc(s_ident16, 1)
            dve.wait_ge(s_const, 3)

            def split_weights(n):
                if n == 0:
                    dve.wait_ge(s_ffn_w, 48)
                    c.do(v.tensor_copy(gw_hi[:, :], gw[:, :]))
                    c.wait()
                    c.do(v.tensor_tensor(gw_lo[:, :], gw[:, :], gw_hi[:, :], ALU.subtract))
                v.tensor_copy(w_hi[:, n, :], w_raw[:, n, :]).then_inc(s_split, 1)
                dve.wait_ge(s_split, 2 * n + 1)
                v.tensor_tensor(w_lo[:, n, :], w_raw[:, n, :], w_hi[:, n, :], ALU.subtract).then_inc(s_split, 1)

            def moments_of(st, src, s_mom, mom, var, ready):
                for t in range(T):
                    st.do(v.bn_stats(s_mom[:, t, :], src(t)))
                st.wait()
                st.do(v.tensor_copy(held_dve[:, :], half[:, 0:1]))
                for t in range(T):
                    st.do(v.bn_aggr(mom[:, t, :], s_mom[:, t, :]))
                st.wait()
                v.tensor_scalar(var[:, :], mom[:, :, 1], LN_EPS, None, ALU.add).then_inc(ready, 1)

            def normalised(st, dst, src, mom, r):
                for t in range(T):
                    st.do(v.tensor_scalar(dst(t), src(t), mom[:, t, 0:1], r[:, t:t + 1],
                                          ALU.subtract, ALU.mult))

            def prep_ln(b):
                st = Steps(dve, s_prep, b, PREP_STEPS)
                dve.wait_ge(s_x if some(b) else s_x0, 16)
                moments_of(st, lambda t: tile_of(stream, b, t), stats, moments, var_eps, s_var)
                return st

            def prep_xn(b, st):
                dve.wait_ge(s_rstd, b + 1)
                for t in range(T):
                    ins = v.tensor_scalar(xn[:, t, :], tile_of(stream, b, t), moments[:, t, 0:1],
                                          rstd[:, t:t + 1], ALU.subtract, ALU.mult)
                    if t < T - 1:
                        st.do(ins)
                st.wait()
                ins.then_inc(s_xn, 1)

            def prep_squares(b, st, uses):
                dve.wait_ge(s_free, uses["qkv3"] + 1)
                st.do(v.tensor_tensor(squares[:, :, :], qkv[:, :, 0:2 * C], qkv[:, :, 0:2 * C], ALU.mult))
                st.wait()
                st.do(v.reduce_sum(ssq[:, :], squares[:, :, :].rearrange("p t (h c) -> p (t h) c", c=HD), AX.X))
                st.wait()
                v.tensor_scalar(msq[:, :], ssq[:, :], 1.0 / HD, None, ALU.mult).then_inc(s_msq, 1)

            def prep_norm(b, st):
                dve.wait_ge(s_rms, b + 1)
                st.do(v.tensor_scalar(rms_eps[:, :], rms[:, :], QK_EPS, None, ALU.add))
                st.wait()
                st.do(v.reciprocal(inv[:, :], rms_eps[:, :]))
                st.wait()
                by_head = inv[:, :].rearrange("p (t h a) -> p t h a", t=T, a=1)
                for dst, first, h0 in ((qn[:, :, :].rearrange("p (t h) c -> p t h c", t=T), 0, 0),
                                       (kn[:, :, :].rearrange("p t (h c) -> p t h c", c=HD), C, H)):
                    st.do(v.tensor_tensor(dst, qkv[:, :, first:first + C].rearrange("p t (h c) -> p t h c", c=HD),
                                          spread(by_head[:, :, h0:h0 + H, :], 3, HD), ALU.mult))
                st.wait()
                st.do(v.tensor_tensor(kw[:, :, :].rearrange("p (t h) c -> p t (h c)", t=T), kn[:, :, :],
                                      spread(qks[:, :].rearrange("p (a n) -> p a n", a=1), 1, T), ALU.mult))

            def prep_stack(b, st):
                st.wait()
                q2 = spread(qn[:, :, :].rearrange("p n (a c) -> p n a c", a=1), 2, 2)
                k2 = spread(kw[:, :, :].rearrange("p n (a c) -> p n a c", a=1), 2, 2)
                q_hi, q_lo = stack[:, 0, :, 0, :, :], stack[:, 0, :, 1, :, :]
                k_hi, k_lo = stack[:, 1, :, :, 0, :], stack[:, 1, :, :, 1, :]
                st.do(v.tensor_copy(q_hi, q2))
                st.do(v.tensor_copy(k_hi, k2))
                st.wait()
                st.do(v.tensor_tensor(q_lo, q2, q_hi, ALU.subtract))
                st.wait()
                v.tensor_tensor(k_lo, k2, k_hi, ALU.subtract).then_inc(s_stack, 1)
                assert st.n == PREP_STEPS, st.n

            PREP_STEPS = 9 + 3 + 2 + 2 + 2 + 1 + 3

            def o_copy(b, g, uses):
                dve.wait_ge(s_pv, b * UNITS + (g + 1) * T)
                if g > 0:
                    dve.wait_ge(s_full, uses[f"oT{g - 1}"] + 1)
                v.tensor_copy(oT[:, :], o_bank[:, :]).then_inc(s_o, 1)

            def o_norm(b, g, uses):
                dve.wait_ge(s_full, uses[f"oT{g}"] + 1)
                view = misc[:, :].rearrange("p (t j c) -> p t j c", t=T, c=32)
                v.reciprocal(recip[:, :, :], view[:, :, :, HD]).then_inc(s_attn, 1)
                dve.wait_ge(s_attn, b * G + g + 1)
                v.tensor_tensor(attn[:, :, 32 * g:32 * g + 32].rearrange("p t (j c) -> p t j c", c=HD),
                                view[:, :, :, 0:HD],
                                spread(recip[:, :, :].rearrange("p t (j a) -> p t j a", a=1), 3, HD),
                                ALU.mult).then_inc(s_free, 1)

            POST_STEPS = 3 + (2 * 2 + 2 + 2) * T + 2 + (T + 1) + (2 * T + 1) + (4 + 2 * T + 1)

            def post_z(b, uses):
                st = Steps(dve, s_post, b, POST_STEPS)
                dve.wait_ge(s_full, uses["proj"] + 1)
                v.tensor_tensor(z[:, :, :], misc[:, :].rearrange("p (t c) -> p t c", t=T),
                                spread(bproj_sb[:, :].rearrange("p (a c) -> p a c", a=1), 1, T),
                                ALU.add).then_inc(s_free, 1)
                dve.wait_ge(s_free, uses["proj"] + 1)
                moments_of(st, lambda t: z[:, t, :], p_stats, p_moments, p_var, s_pvar)
                return st

            def post_x1(b, st):
                dve.wait_ge(s_prstd, 3 * b + 1)
                normalised(st, lambda t: zn[:, t, :], lambda t: z[:, t, :], p_moments, p_rstd)
                st.wait()
                for t in range(T):
                    st.do(v.tensor_tensor(x1[:, t, :], tile_of(stream, b, t), zn[:, t, :], ALU.add))
                st.wait()
                moments_of(st, lambda t: x1[:, t, :], p_stats, p_moments, p_var, s_pvar)

            def post_xin(b, st):
                dve.wait_ge(s_prstd, 3 * b + 2)
                normalised(st, lambda t: xin[:, t, :], lambda t: x1[:, t, :], p_moments, p_rstd)
                for t in range(T):
                    st.do(v.tensor_copy(tile_of(stream, b, t), x1[:, t, :]))
                st.wait()
                st.do(v.tensor_tensor(xin_sq[:, :, :], xin[:, :, :], xin[:, :, :], ALU.mult))
                st.wait()
                st.do(v.reduce_sum(e_sum[:, :], xin_sq[:, :, :], AX.X))
                st.wait()
                v.tensor_scalar(p_var[:, :], e_sum[:, :], 1.0 / C, FFN_EPS, ALU.mult, ALU.add).then_inc(s_pvar, 1)

            def post_y(b, st):
                dve.wait_ge(s_prstd, 3 * b + 3)
                for t in range(T):
                    st.do(v.scalar_tensor_tensor(out=y[:, t, :], in0=xin[:, t, :], scalar=p_rstd[:, t:t + 1],
                                                 in1=rms_sb[:, :], op0=ALU.mult, op1=ALU.mult))
                st.wait()
                st.do(v.tensor_copy(y_split[:, 0, :, :], y[:, :, :]))
                st.wait()
                v.tensor_tensor(y_split[:, 1, :, :], y[:, :, :], y_split[:, 0, :, :],
                                ALU.subtract).then_inc(s_y, 1)

            def post_top(b, st, uses):
                dve.wait_ge(s_full, uses["logits"] + 1)
                v.tensor_copy(logit[:, :, :], misc[:, 0:T * E].rearrange("p (t e) -> p t e", t=T)
                              ).then_inc(s_free, 1)
                dve.wait_ge(s_free, uses["logits"] + 1)
                st.do(v.tensor_copy(held_dve[:, :], half[:, 0:1]))
                for t in range(T):
                    st.do(v.max(top[:, t, :], logit[:, t, :]))
                st.wait()
                v.tensor_tensor(gap[:, :], top[:, :, 1], top[:, :, 0], ALU.subtract).then_inc(s_gap, 1)
                for t in range(T):
                    st.do(v.max_index(top_at[:, t, :], top[:, t, :], logit[:, t, :]))
                st.wait()
                st.do(v.tensor_copy(top_no[:, :, :], top_at[:, :, 0:2]))

            def post_route(b, st):
                dve.wait_ge(s_e2, b + 1)
                st.do(v.tensor_scalar(e_sum[:, :], e2[:, :], 1.0, None, ALU.add))
                st.wait()
                st.do(v.reciprocal(e_inv[:, :], e_sum[:, :]))
                st.wait()
                st.do(v.tensor_scalar(w_top[:, 0, :], e_inv[:, :], 0.5, None, ALU.mult))
                st.wait()
                st.do(v.tensor_tensor(w_top[:, 1, :], w_top[:, 0, :], e2[:, :], ALU.mult))
                st.wait()
                for n, dst in enumerate((w_a, w_b)):
                    for t in range(T):
                        st.do(v.tensor_scalar(dst[:, t, :], expert_no[:, :], top_no[:, t, n:n + 1],
                                              w_top[:, n, t:t + 1], ALU.is_equal, ALU.mult))
                st.wait()
                st.do(v.tensor_tensor(batch_of(route, b), w_a[:, :, :].rearrange("p t e -> p (t e)"),
                                      w_b[:, :, :].rearrange("p t e -> p (t e)"), ALU.add))
                assert st.n == POST_STEPS, st.n
                st.wait()

            def hidden(b, k):
                rows = PARTS[k % len(PARTS)][1]
                dve.wait_ge(s_tanh, b * TILES + k + 1)
                if k >= 2:
                    dve.wait_ge(s_hid, b * TILES + k - 1)
                elif some(b):
                    dve.wait_ge(s_hid, b * TILES)
                v.scalar_tensor_tensor(out=act2[0:rows, k % 2, :], in0=th[0:rows, k % 2, :], scalar=1.0,
                                       in1=up[0:rows, :], op0=ALU.add, op1=ALU.mult).then_inc(s_act, 1)
                dve.wait_ge(s_act, b * TILES + k + 1)
                dve.wait_ge(s_gate, b * TILES + k + 1)
                if k >= HR:
                    dve.wait_ge(s_dn, b * TILES + k - HR + 1)
                elif some(b):
                    dve.wait_ge(s_dn, b * TILES)
                v.tensor_tensor(hid[0:rows, k % HR, :], act2[0:rows, k % 2, :], gate[0:rows, :],
                                ALU.mult).then_inc(s_hid, 1)

            def combine(b, e):
                dve.wait_ge(s_dn, b * TILES + (e + 1) * len(PARTS))
                if e == 0:
                    dve.wait_ge(s_route_now, b + 1)
                else:
                    dve.wait_ge(s_comb, b * E + e)
                for t in range(T):
                    before = xin if e == 0 else acc
                    ins = v.scalar_tensor_tensor(out=acc[:, t, :], in0=down[:, t * C:(t + 1) * C],
                                                 scalar=route_now[:, t * E + e:t * E + e + 1],
                                                 in1=before[:, t, :], op0=ALU.mult, op1=ALU.add)
                ins.then_inc(s_comb, 1)

            FIN_STEPS = 9 + 4

            def final(b):
                dve.wait_ge(s_comb, (b + 1) * E)
                st = Steps(dve, s_fin, b, FIN_STEPS)
                moments_of(st, lambda t: acc[:, t, :], f_stats, f_moments, f_var, s_fvar)
                dve.wait_ge(s_frstd, b + 1)
                normalised(st, lambda t: fn[:, t, :], lambda t: acc[:, t, :], f_moments, f_rstd)
                st.wait()
                if some(b):
                    dve.wait_ge(s_out, 16 * b)
                for t in range(T):
                    ins = v.tensor_tensor(result[:, t, :], fn[:, t, :], tile_of(stream, b, t), ALU.add)
                ins.then_inc(s_result, 1)

            def run(att, ffn, prep):
                if att is None and ffn is None:
                    st = prep_ln(prep)
                    prep_xn(prep, st)
                    prep_squares(prep, st, Uses(None, True))
                    prep_norm(prep, st)
                    prep_stack(prep, st)
                    return
                uses = Uses(att, prep is not None) if att is not None else None
                if ffn is not None:
                    v.tensor_copy(route_now[:, :], batch_of(route, ffn)).then_inc(s_route_now, 1)
                for s in range(SLOTS):
                    if prep is not None:
                        if s == 0:
                            st_prep = prep_ln(prep)
                        elif s == 1:
                            prep_xn(prep, st_prep)
                        elif s == 7:
                            prep_squares(prep, st_prep, uses)
                        elif s == 14:
                            prep_norm(prep, st_prep)
                        elif s == 15:
                            prep_stack(prep, st_prep)
                    if ffn is not None:
                        hidden(ffn, s)
                        if s >= 4 and (s - 4) % len(PARTS) == 0:
                            combine(ffn, (s - 4) // len(PARTS))
                    elif att is not None and s in (3, 6):
                        split_weights((s - 3) // 3)
                    if att is not None:
                        if s >= 4 and s % T == 0 and s // T <= G:
                            o_copy(att, s // T - 1, uses)
                        if s >= 5 and s % T == 1 and s // T <= G:
                            o_norm(att, s // T - 1, uses)
                        if s == 19:
                            st_post = post_z(att, uses)
                        elif s == 20:
                            post_x1(att, st_post)
                        elif s == 21:
                            post_xin(att, st_post)
                        elif s == 22:
                            post_y(att, st_post)
                        elif s == 23:
                            post_top(att, st_post, uses)
                            post_route(att, st_post)
                if ffn is not None:
                    combine(ffn, E - 1)
                    final(ffn)

            iterations(dve, run)


def kernel(L0_attn_x, L0_attn_Wqkv, L0_attn_Wproj, L0_attn_bproj, L0_attn_q_scale, L0_attn_k_scale,
           L0_ffn_gate_w, L0_ffn_rms_w, L0_ffn_W1, L0_ffn_W2, L0_ffn_W3):
    import numpy as np
    import concourse.bacc as bacc
    from concourse.bass_utils import run_bass_kernel_spmd

    def rows(a, repeat=1):
        return np.ascontiguousarray(np.broadcast_to(np.tile(np.asarray(a), repeat), (P, a.shape[0] * repeat)))

    arrays = {
        "x": np.ascontiguousarray(L0_attn_x),
        "wqkv": np.ascontiguousarray(L0_attn_Wqkv),
        "wproj": np.ascontiguousarray(L0_attn_Wproj),
        "bproj": rows(L0_attn_bproj),
        "q_scale": rows(L0_attn_q_scale, H),
        "k_scale": rows(L0_attn_k_scale, H),
        "gate_wT": np.ascontiguousarray(np.asarray(L0_ffn_gate_w).T),
        "rms_w": rows(L0_ffn_rms_w),
        "w1T": np.ascontiguousarray(np.asarray(L0_ffn_W1).reshape(E * DE, C).T),
        "w2T": np.ascontiguousarray(np.asarray(L0_ffn_W2).reshape(E * DE, C).T),
        "w3T": np.ascontiguousarray(np.asarray(L0_ffn_W3).transpose(0, 2, 1)),
    }
    nc = bacc.Bacc("TRN2", target_bir_lowering=False, num_devices=1)
    args = [nc.dram_tensor(f"in_{name}", a.shape, mybir.dt.from_np(a.dtype), kind="ExternalInput").ap()
            for name, a in arrays.items()]
    out = nc.dram_tensor("out_dram", (B, N, C), F32, kind="ExternalOutput").ap()
    layers(nc, *args, out)
    r = run_bass_kernel_spmd(nc, [{f"in_{name}": a for name, a in arrays.items()}], core_ids=[0])
    return r.results[0]["out_dram"]
```

```python
import concourse.bass as bass
from concourse import mybir
from contextlib import ExitStack

F32 = mybir.dt.float32
F16 = mybir.dt.float16
U32 = mybir.dt.uint32
ALU = mybir.AluOpType
ACT = mybir.ActivationFunctionType
AX = mybir.AxisListType

P = 128
B, N, C = 4, 512, 128
T = N // P
H, HD = 16, 8
G = H // 4
E, DE = 8, 352
PARTS = [(0, 128), (128, 128), (256, 96)]
TILES = E * len(PARTS)
UNITS = G * T
SLOTS = TILES
SAFE = 80.0
MAGIC = 0x5F3759DF
LN_EPS, QK_EPS, FFN_EPS = 1e-5, 1e-8, 1e-6

MISC = {0: ["logits"], 4: ["xT"], 5: ["oT0", "qkv0"], 6: ["qkv1"], 7: ["qkv2"], 8: ["qkv3"], 9: ["oT1"],
        13: ["oT2"], 17: ["oT3", "stack0"], 18: ["aT", "stack1"], 19: ["proj", "stack2"], 20: ["stack3"],
        23: ["yT"]}
PREP_LN, PREP_XN, PREP_SQUARES, PREP_NORM, PREP_HIGH, PREP_LOW = 3, 4, 9, 11, 13, 15
POST_Z, POST_X1, POST_V, POST_Y = 19, 20, 21, 22
ROUTE, FINAL = 2, 1
CUT = 3
PREP_USES = ["xT", "qkv0", "qkv1", "qkv2", "qkv3", "stack0", "stack1", "stack2", "stack3"]
ALL_USES = [name for slot in sorted(MISC) for name in MISC[slot]]
POST_USES = [name for name in ALL_USES if name not in PREP_USES]
N_PREP, N_ALL = len(PREP_USES), len(ALL_USES)
assert ALL_USES[0] == "logits"


CREDIT = 3


def upto(n):
    return n + CREDIT


def spread(ap, axis, n):
    shape = list(ap.shape)
    shape[axis] = n
    return ap.broadcast_to(shape)


class Uses:

    def __init__(self, b, prep):
        self.b, self.alone = b, b is None
        self.base = 0 if b is None else b * N_ALL + N_PREP - 1
        self.names = PREP_USES if b is None else ALL_USES if prep else POST_USES

    def __getitem__(self, name):
        if isinstance(self.b, int) and self.b == B:
            return self.base - N_PREP + self.names.index(name)
        return self.base + self.names.index(name)


class Steps:

    def __init__(self, eng, sem, b, per):
        self.eng, self.sem, self.b, self.per, self.n = eng, sem, b, per, 0

    def do(self, instruction):
        self.n += 1
        assert self.n <= self.per
        instruction.then_inc(self.sem, 1)

    def wait(self):
        self.eng.wait_ge(self.sem, self.b * self.per + self.n)


def layers(nc, x, wqkv, wproj, bproj, q_scale, k_scale, gate_wT, rms_w, w1T, w2T, w3T, out):
    with ExitStack() as ctx:
        def sb(name, shape, dt=F32):
            return ctx.enter_context(nc.sbuf_tensor(name, shape, dt))

        def sem(name):
            return ctx.enter_context(nc.semaphore(name))

        stream = sb("stream", [P, B * T, C])
        wqkv_sb = sb("wqkv_sb", [P, 3 * C])
        wproj_sb = sb("wproj_sb", [P, C])
        bproj_sb = sb("bproj_sb", [P, C])
        rms_sb = sb("rms_sb", [P, C])
        qs_sb = sb("qs_sb", [P, H * HD])
        ks_sb = sb("ks_sb", [P, H * HD])
        qks = sb("qks", [P, H * HD])
        w_raw = sb("w_raw", [P, 2, E * DE])
        w_hi = sb("w_hi", [P, 2, E * DE], F16)
        w_lo = sb("w_lo", [P, 2, E * DE], F16)
        w3 = sb("w3", [P, E, 3, C])
        gw = sb("gw", [P, E])
        gw_hi = sb("gw_hi", [P, E], F16)
        gw_lo = sb("gw_lo", [P, E], F16)
        ident = sb("ident", [P, P])
        ident16 = sb("ident16", [P, P], F16)
        expert_no = sb("expert_no", [P, E])
        half = sb("half", [P, 1])
        magic = sb("magic", [P, T * 2 * H], U32)
        neg_half = sb("neg_half", [P, T])
        qks_neg = sb("qks_neg", [P, H * HD])
        qks_max = sb("qks_max", [P, 1])
        shift0 = sb("shift0", [P, 1])
        shift = sb("shift", [P, 1])
        held_dve = sb("held_dve", [P, 1])
        warm = sb("warm", [P, 1])
        held_pool = sb("held_pool", [P, 1])

        stats = sb("stats", [P, T, 6])
        moments = sb("moments", [P, T, 2])
        var_eps = sb("var_eps", [P, T])
        rstd = sb("rstd", [P, T])
        xn = sb("xn", [P, T, C])
        xnT = sb("xnT", [P, N])
        qkv = sb("qkv", [P, T, 3 * C])
        squares = sb("squares", [P, T, 2 * C])
        ssq = sb("ssq", [P, T * 2 * H])
        msq = sb("msq", [P, T * 2 * H])
        guess = sb("guess", [P, 2, T * 2 * H], U32)
        newton = sb("newton", [P, 5, T * 2 * H])
        rms = sb("rms", [P, T * 2 * H])
        rms_eps = sb("rms_eps", [P, T * 2 * H])
        inv = sb("inv", [P, T * 2 * H])
        qn = sb("qn", [P, T * H, HD])
        kn = sb("kn", [P, T, H * HD])
        kw = sb("kw", [P, T * H, HD])
        stack = sb("stack", [P, 2, T * H, 2, 2, HD], F16)
        qkT = sb("qkT", [P, 2 * G, N], F16)
        v_ext = sb("v_ext", [P, T * H, 32])

        PR = 8
        probs = sb("probs", [P, PR, N])
        oT = sb("oT", [P, N])
        recip = sb("recip", [P, T, 4])
        attn = sb("attn", [P, T, C])
        attnT = sb("attnT", [P, N])
        z = sb("z", [P, T, C])
        zn = sb("zn", [P, T, C])
        p_stats = sb("p_stats", [P, T, 6])
        p_moments = sb("p_moments", [P, T, 2])
        p_var = sb("p_var", [P, T])
        p_rstd = sb("p_rstd", [P, T])
        x1 = sb("x1", [P, T, C])
        xin = sb("xin", [P, T, C])
        xin_ms = sb("xin_ms", [P, 4, T])
        y_rstd = sb("y_rstd", [P, T])
        ffn_eps = sb("ffn_eps", [P, T])
        yv = sb("yv", [P, T, C])
        y_split = sb("y_split", [P, 2, T, C], F16)
        yT = sb("yT", [P, B, 2 * N], F16)
        logit = sb("logit", [P, T, E])
        top = sb("top", [P, T, E])
        top_at = sb("top_at", [P, T, E], U32)
        top_no = sb("top_no", [P, T, 2])
        gap = sb("gap", [P, T])
        e2 = sb("e2", [P, T])
        e_sum = sb("e_sum", [P, T])
        e_inv = sb("e_inv", [P, T])
        w_top = sb("w_top", [P, 2, T])
        w_a = sb("w_a", [P, T, E])
        w_b = sb("w_b", [P, T, E])
        route = sb("route", [P, T * E])

        th = sb("th", [P, 2, N])
        act2 = sb("act2", [P, 2, N])
        HR = 3
        hid = sb("hid", [P, HR, N])
        acc = sb("acc", [P, T, C])
        f_stats = sb("f_stats", [P, T, 6])
        f_moments = sb("f_moments", [P, T, 2])
        f_var = sb("f_var", [P, T])
        f_rstd = sb("f_rstd", [P, T])
        fn = sb("fn", [P, T, C])
        result = sb("result", [P, T, C])

        bank = [ctx.enter_context(nc.psum_tensor(f"bank{i}", [P, N], F32)) for i in range(8)]
        o_bank, misc = bank[2], bank[7]
        def score_banks(ffn):
            return bank[0:2] if ffn is not None else bank[0:2] + bank[3:5]

        up_banks = bank[3:5]

        def gate_banks(att):
            return bank[5:6] if att is not None else [bank[5], bank[0]]

        def down_banks(att):
            return bank[6:7] if att is not None else [bank[6], bank[1]]

        s_wqkv = sem("wqkv_in")
        s_x0, s_x, s_small, s_attn_w, s_ffn_w, s_w3 = (
            sem(n) for n in ("x0_in", "x_in", "small_in", "attn_w_in", "ffn_w_in", "w3_in"))
        s_id0, s_ident, s_ident16, s_const, s_vzero = (
            sem(n) for n in ("ident_zero", "ident", "ident16", "constants", "v_zero"))
        s_c = sem("constant_steps")
        s_split = sem("weights_split")
        s_full, s_free = sem("misc_full"), sem("misc_free")
        s_prep = sem("prep_steps")
        s_var, s_rstd = sem("prep_var"), sem("prep_rstd")
        s_xn, s_msq, s_rms = sem("xn_ready"), sem("msq_ready"), sem("rms_ready")
        s_qkn, s_high = sem("qk_normed"), sem("high_parts")
        s_stack, s_v = sem("stack_ready"), sem("v_ready")
        s_qk, s_exp, s_pv, s_o, s_attn = (
            sem(n) for n in ("scores_done", "probs_done", "pv_done", "o_copied", "attn_steps"))
        s_post, s_pvar, s_prstd, s_y = (
            sem(n) for n in ("post_steps", "post_var", "post_rstd", "y_ready"))
        s_ms = sem("mean_square_steps")
        s_gap, s_e2 = sem("gap_ready"), sem("e2_ready")
        s_up, s_gate, s_tanh, s_act, s_hid, s_dn, s_comb = (
            sem(n) for n in ("up_done", "gate_done", "tanh_done", "act_done", "hid_done", "down_done", "combined"))
        s_route, s_yv, s_yrstd, s_yhigh = sem("route_steps"), sem("yv_ready"), sem("y_rstd"), sem("y_high")
        s_fpool = sem("final_pool_steps")
        s_fin, s_fvar, s_frstd, s_result, s_out = (
            sem(n) for n in ("final_steps", "final_var", "final_rstd", "result_ready", "out_written"))

        block = ctx.enter_context(nc.Block())

        def misc_bank(name, att):
            if att is None and name not in ("xT", "logits"):
                return bank[int(name[-1]) + (4 if name.startswith("stack") else 0)]
            return misc

        def uses_of(att, prep, slots):
            return Uses(B, True) if att is None else Uses(att, prep is not None)

        def wanted(name, att, ffn, prep):
            stage = ffn if name == "logits" else prep if name in PREP_USES else att
            return stage is not None

        def tile_of(ap, b, t):
            if isinstance(b, int):
                return ap[:, b * T + t, :]
            return ap[:, bass.ds(b * T + t, 1), :].rearrange("p a c -> p (a c)")

        def batch_of(ap, b):
            if isinstance(b, int):
                return ap[:, b, :]
            return ap[:, bass.ds(b, 1), :].rearrange("p a n -> p (a n)")

        def some(b):
            return not isinstance(b, int) or b > 0

        def iterations(start, run, eng):
            start()
            run(0, None, 1, None, range(SLOTS))
            run(1, 0, 2, None, range(CUT))
            with eng.Fori(1, B - 1) as b:
                run(b, b - 1, b + 1, None, range(CUT, SLOTS))
                run(b + 1, b, None, b - 1, range(CUT))
            run(B - 1, B - 2, None, None, range(CUT, SLOTS))
            run(None, B - 1, None, B - 2, range(SLOTS))

        @block.sync
        def _(sp):
            rows = x.rearrange("b (t p) c -> p (b t) c", p=P)
            sp.dma_start(stream[:, 0:T, :], rows[:, 0:T, :]).then_inc(s_x0, 16)
            sp.dma_start(wqkv_sb[:, :], wqkv).then_inc(s_wqkv, 16)
            sp.dma_start(qs_sb[:, :], q_scale).then_inc(s_small, 16)
            sp.dma_start(ks_sb[:, :], k_scale).then_inc(s_small, 16)
            sp.dma_start(stream[:, T:B * T, :], rows[:, T:B * T, :]).then_inc(s_x, 16)
            sp.dma_start(wproj_sb[:, :], wproj).then_inc(s_attn_w, 16)
            sp.dma_start(bproj_sb[:, :], bproj).then_inc(s_attn_w, 16)
            sp.dma_start(rms_sb[:, :], rms_w).then_inc(s_attn_w, 16)
            sp.dma_start(gw[:, :], gate_wT).then_inc(s_ffn_w, 16)
            sp.dma_start(w_raw[:, 0, :], w1T).then_inc(s_ffn_w, 16)
            sp.dma_start(w_raw[:, 1, :], w2T).then_inc(s_ffn_w, 16)
            for i, (first, rows_i) in enumerate(PARTS):
                sp.dma_start(w3[0:rows_i, :, i, :],
                             w3T[:, first:first + rows_i, :].rearrange("e p m -> p e m")).then_inc(s_w3, 16)

            def store(b):
                sp.wait_ge(s_result, upto(b + 1))
                dst = out[b] if isinstance(b, int) else out[bass.ds(b, 1)].rearrange("a n c -> (a n) c")
                sp.dma_start(dst.rearrange("(t p) c -> p t c", p=P), result[:, :, :]).then_inc(s_out, 16)

            def run(att, ffn, prep, end, slots):
                if end is not None:
                    store(end)

            iterations(lambda: None, run, sp)
            store(B - 1)
            sp.wait_ge(s_out, upto(16 * B))

        @block.gpsimd
        def _(pool):
            pool.memset(ident[:, :], 0.0).then_inc(s_id0, 1)
            pool.memset(neg_half[:, :], -0.5).then_inc(s_const, 1)
            pool.memset(half[:, :], 0.5).then_inc(s_const, 1)
            pool.memset(magic[:, :], MAGIC + 1).then_inc(s_const, 1)
            pool.memset(ffn_eps[:, :], FFN_EPS).then_inc(s_const, 1)
            pool.wait_ge(s_id0, 1)
            pool.affine_select(out=ident[:, :], in_=ident[:, :], compare_op=ALU.not_equal, fill=1.0,
                               base=0, pattern=[[-1, P]], channel_multiplier=1).then_inc(s_ident, 1)
            pool.iota(expert_no[:, :], [[1, E]], base=0, channel_multiplier=0,
                      allow_small_or_imprecise_dtypes=True).then_inc(s_const, 1)
            pool.memset(v_ext[:, :, :], 0.0).then_inc(s_vzero, 1)
            pool.wait_ge(s_vzero, 1)
            pool.memset(v_ext[:, :, HD:HD + 1], 1.0).then_inc(s_vzero, 1)
            pool.wait_ge(s_vzero, 2)
            pool.wait_ge(s_const, 5)

            def norm_power(b, ready, done, src, dst, n, of):
                pool.wait_ge(ready, b * of + n + 1)
                pool.tensor_tensor(dst[:, :], src[:, :], neg_half[:, :], ALU.pow).then_inc(done, 1)

            def prep_v(b, uses):
                if some(b):
                    pool.wait_ge(s_pv, b * UNITS)
                pool.wait_ge(s_free, uses["qkv3"] + 1)
                pool.tensor_tensor(held_pool[:, :], half[:, 0:1], half[:, 0:1], ALU.mult)
                for t in range(T):
                    ins = pool.tensor_copy(v_ext[:, t * H:(t + 1) * H, 0:HD],
                                           qkv[:, t, 2 * C:3 * C].rearrange("p (h c) -> p h c", c=HD))
                ins.then_inc(s_v, 1)

            def post(b):
                for n in range(2):
                    norm_power(b, s_pvar, s_prstd, p_var, p_rstd, n, 2)
                st = Steps(pool, s_ms, b, 4)
                pool.wait_ge(s_prstd, b * 2 + 2)
                st.do(pool.tensor_tensor(xin_ms[:, 0, :], p_rstd[:, :], p_rstd[:, :], ALU.mult))
                st.wait()
                st.do(pool.tensor_tensor(xin_ms[:, 1, :], xin_ms[:, 0, :], p_moments[:, :, 1], ALU.mult))
                st.wait()
                st.do(pool.tensor_tensor(xin_ms[:, 2, :], xin_ms[:, 1, :], ffn_eps[:, :], ALU.add))
                st.wait()
                st.do(pool.tensor_tensor(xin_ms[:, 3, :], xin_ms[:, 2, :], neg_half[:, :], ALU.pow))
                st.wait()
                pool.tensor_tensor(y_rstd[:, :], xin_ms[:, 3, :], p_rstd[:, :], ALU.mult).then_inc(s_yrstd, 1)

            def final(b):
                st = Steps(pool, s_fpool, b, T + 1)
                norm_power(b, s_fvar, s_frstd, f_var, f_rstd, 0, 1)
                pool.wait_ge(s_frstd, b + 1)
                pool.tensor_tensor(held_pool[:, :], half[:, 0:1], half[:, 0:1], ALU.mult)
                for t in range(T):
                    st.do(pool.tensor_scalar(fn[:, t, :], acc[:, t, :], f_moments[:, t, 0:1],
                                             f_rstd[:, t:t + 1], ALU.subtract, ALU.mult))
                pool.wait_ge(s_out, upto(16 * b))
                st.wait()
                st.do(pool.tensor_tensor(held_pool[:, :], half[:, 0:1], half[:, 0:1], ALU.mult))
                for t in range(T):
                    ins = pool.tensor_tensor(result[:, t, :], fn[:, t, :], tile_of(stream, b, t), ALU.add)
                ins.then_inc(s_result, 1)

            def start():
                norm_power(0, s_var, s_rstd, var_eps, rstd, 0, 1)
                prep_v(0, Uses(None, True))

            def run(att, ffn, prep, end, slots):
                if FINAL in slots and end is not None:
                    final(end)
                if PREP_LN in slots and prep is not None:
                    norm_power(prep, s_var, s_rstd, var_eps, rstd, 0, 1)
                    prep_v(prep, Uses(att, True))
                if POST_Z in slots and att is not None:
                    post(att)

            iterations(start, run, pool)
            final(B - 1)

        @block.tensor
        def _(pe):
            pe.wait_ge(s_ident, 1)
            pe.wait_ge(s_wqkv, 16)
            pe.wait_ge(s_ident16, 1)

            def fill(uses, name):
                n = uses[name]
                if uses.alone:
                    n = min(n, 1)
                if not isinstance(n, int) or n > 0:
                    pe.wait_ge(s_free, n)

            def transposes(dst, src, what):
                for t in range(T):
                    ins = pe.transpose(dst[:, t * P:(t + 1) * P], src(t), what[:, :])
                return ins

            def misc_use(name, uses, att, prep, y_ffn=None):
                misc = misc_bank(name, att)
                misc16 = misc[:, :].bitcast(F16)
                if name == "xT":
                    pe.wait_ge(s_xn, prep + 1)
                    fill(uses, name)
                    ins = transposes(misc, lambda t: xn[:, t, :], ident)
                elif name.startswith("qkv"):
                    t = int(name[3:])
                    fill(uses, name)
                    ins = pe.matmul(misc[:, 0:3 * C], xnT[:, t * P:(t + 1) * P], wqkv_sb[:, :],
                                    start=True, stop=True)
                elif name.startswith("stack"):
                    t = int(name[5:])
                    pe.wait_ge(s_stack, prep + 1)
                    fill(uses, name)
                    for qk in range(2):
                        for g in range(G):
                            at = (qk * G + g) * P
                            src = stack[:, qk, t * H + 4 * g:t * H + 4 * g + 4, :, :, :]
                            ins = pe.transpose(misc16[:, at:at + P],
                                               src.rearrange("p h a b c -> p (h a b c)"), ident16[:, :])
                elif name.startswith("oT"):
                    g = int(name[2:])
                    pe.wait_ge(s_o, att * G + g + 1)
                    fill(uses, name)
                    ins = transposes(misc, lambda t: oT[:, t * P:(t + 1) * P], ident)
                elif name == "aT":
                    fill(uses, name)
                    pe.wait_ge(s_free, uses["oT3"] + 1)
                    ins = transposes(misc, lambda t: attn[:, t, :], ident)
                elif name == "proj":
                    fill(uses, name)
                    pe.wait_ge(s_free, uses["aT"] + 1)
                    for t in range(T):
                        ins = pe.matmul(misc[:, t * C:(t + 1) * C], attnT[:, t * P:(t + 1) * P],
                                        wproj_sb[:, :], start=True, stop=True)
                elif name == "yT":
                    pe.wait_ge(s_y, att + 1)
                    fill(uses, name)
                    for s in range(2):
                        for t in range(T):
                            at = s * N + t * P
                            ins = pe.transpose(misc16[:, at:at + P], y_split[:, s, t, :], ident16[:, :])
                elif name == "logits":
                    fill(uses, name)
                    for t in range(T):
                        for i, (s, w) in enumerate(((0, gw_hi), (0, gw_lo), (1, gw_hi), (1, gw_lo))):
                            at = s * N + t * P
                            ins = pe.matmul(misc[:, t * E:(t + 1) * E], y_ffn[:, at:at + P], w[:, :],
                                            start=i == 0, stop=i == 3)
                ins.then_inc(s_full, 1)

            def scores(b, u, pair, banks):
                g, m = divmod(u, T)
                for j in (2 * pair, 2 * pair + 1):
                    n = 4 * u + j
                    if n >= len(banks):
                        pe.wait_ge(s_exp, b * 4 * UNITS + n - len(banks) + 1)
                    elif some(b):
                        pe.wait_ge(s_exp, b * 4 * UNITS)
                    r = slice(32 * j, 32 * j + 32)
                    pe.matmul(banks[n % len(banks)][:, :], qkT[r, G + g, m * P:(m + 1) * P], qkT[r, g, :],
                              start=True, stop=True).then_inc(s_qk, 1)

            def weighted(b, u):
                g, m = divmod(u, T)
                pe.wait_ge(s_exp, b * 4 * UNITS + 4 * u + 4)
                if u == 0:
                    pe.wait_ge(s_v, b + 1)
                if m == 0 and (g > 0 or some(b)):
                    pe.wait_ge(s_o, b * G + g)
                for j in range(4):
                    ins = pe.matmul(o_bank[32 * j:32 * j + 32, :], v_ext[:, m * H + 4 * g + j, :],
                                    probs[:, (4 * u + j) % PR, :], start=m == 0, stop=m == T - 1,
                                    skip_group_check=True)
                ins.then_inc(s_pv, 1)

            def expand(b, k, which, y_b, banks):
                e, i = divmod(k, len(PARTS))
                at, rows = e * DE + PARTS[i][0], PARTS[i][1]
                dst, done, used = banks[k % len(banks)], (s_up, s_gate)[which], (s_act, s_hid)[which]
                before = k + 1 - len(banks) if which == 0 else max(k + 1 - len(banks), 0)
                pe.wait_ge(used, upto(b * TILES + before))
                hi, lo = (w[:, which, at:at + rows] for w in (w_hi, w_lo))
                pe.matmul(dst[0:rows, :], hi, y_b[:, 0:N], start=True, stop=False)
                pe.matmul(dst[0:rows, :], hi, y_b[:, N:2 * N], start=False, stop=False)
                pe.matmul(dst[0:rows, :], lo, y_b[:, 0:N], start=False, stop=True).then_inc(done, 1)

            def contract(b, k, banks):
                e, i = divmod(k, len(PARTS))
                rows = PARTS[i][1]
                pe.wait_ge(s_hid, upto(b * TILES + k + 1))
                if i == 0:
                    pe.wait_ge(s_comb, upto(b * E + max(e + 1 - len(banks), 0)))
                for t in range(T):
                    ins = pe.matmul(banks[e % len(banks)][:, t * C:(t + 1) * C], hid[0:rows, k % HR, t * P:(t + 1) * P],
                                    w3[0:rows, e, i, :], start=i == 0 and t == 0,
                                    stop=i == len(PARTS) - 1, skip_group_check=True)
                ins.then_inc(s_dn, 1)

            def start():
                for name in PREP_USES:
                    misc_use(name, Uses(None, True), None, 0)
                pe.wait_ge(s_free, N_PREP)

            def run(att, ffn, prep, end, slots):
                uses = uses_of(att, prep, slots)
                s_banks, g_banks, d_banks = score_banks(ffn), gate_banks(att), down_banks(att)
                if ffn is not None:
                    y_ffn = batch_of(yT, ffn)
                    if 0 in slots:
                        pe.wait_ge(s_free, uses["logits"])
                else:
                    y_ffn = None
                if att is None:
                    pe.wait_ge(s_exp, B * 4 * UNITS)
                for s in slots:
                    if att is not None and s < UNITS:
                        scores(att, s, 0, s_banks)
                    if ffn is not None:
                        expand(ffn, s, 0, y_ffn, up_banks)
                        expand(ffn, s, 1, y_ffn, g_banks)
                    if att is not None and s < UNITS:
                        scores(att, s, 1, s_banks)
                    if att is not None and 1 <= s <= UNITS:
                        weighted(att, s - 1)
                    if ffn is not None and s >= 1:
                        contract(ffn, s - 1, d_banks)
                    elif end is not None and s == 0:
                        contract(end, SLOTS - 1, down_banks(0))
                    if ffn is None and s == UNITS + 1:
                        pe.wait_ge(s_attn_w, 48)
                        pe.wait_ge(s_split, 4)
                        pe.wait_ge(s_w3, 48)
                    for name in MISC.get(s, ()):
                        if wanted(name, att, ffn, prep):
                            misc_use(name, uses, att, prep, y_ffn)

            iterations(start, run, pe)
            contract(B - 1, SLOTS - 1, down_banks(None))

        @block.scalar
        def _(act):
            act.wait_ge(s_const, 5)
            act.activation(warm[:, :], half[:, 0:1], ACT.Exp)
            act.wait_ge(s_c, 6)

            def copy_out(uses, name, dst, src):
                act.wait_ge(s_full, uses[name] + 1)
                act.activation(dst, src, ACT.Copy).then_inc(s_free, 1)

            def misc_use(name, uses, att, prep):
                misc = misc_bank(name, att)
                misc16 = misc[:, :].bitcast(F16)
                if name == "xT":
                    copy_out(uses, name, xnT[:, :], misc[:, :])
                elif name.startswith("qkv"):
                    if name == "qkv0" and some(prep):
                        act.wait_ge(s_v, prep)
                    t = int(name[3:])
                    copy_out(uses, name, qkv[:, t, :], misc[:, 0:3 * C])
                elif name.startswith("stack"):
                    t = int(name[5:])
                    copy_out(uses, name, qkT[:, :, t * P:(t + 1) * P],
                             misc16.rearrange("p (a n) -> p a n", n=P))
                elif name == "aT":
                    copy_out(uses, name, attnT[:, :], misc[:, :])
                elif name == "yT":
                    copy_out(uses, name, batch_of(yT, att), misc16)

            def high_parts(b):
                act.wait_ge(s_qkn, b + 1)
                for dst, src in ((stack[:, 0, :, 0, :, :], qn), (stack[:, 1, :, :, 0, :], kw)):
                    ins = act.activation(dst, spread(src[:, :, :].rearrange("p n (a c) -> p n a c", a=1), 2, 2),
                                         ACT.Copy)
                ins.then_inc(s_high, 1)

            def o_copy(b, g, uses):
                act.wait_ge(s_pv, b * UNITS + (g + 1) * T)
                if g > 0:
                    act.wait_ge(s_full, uses[f"oT{g - 1}"] + 1)
                act.activation(oT[:, :], o_bank[:, :], ACT.Copy).then_inc(s_o, 1)

            def exps(b, u, pair, banks):
                for j in (2 * pair, 2 * pair + 1):
                    n = 4 * u + j
                    act.wait_ge(s_qk, b * 4 * UNITS + n + 1)
                    if u >= 2:
                        act.wait_ge(s_pv, b * UNITS + u - 1)
                    elif some(b):
                        act.wait_ge(s_pv, b * UNITS)
                    act.activation(probs[:, n % PR, :], banks[n % len(banks)][:, :], ACT.Exp,
                                   bias=shift[:, :]).then_inc(s_exp, 1)

            def tanh(b, k):
                rows = PARTS[k % len(PARTS)][1]
                act.wait_ge(s_up, b * TILES + k + 1)
                act.wait_ge(s_act, upto(b * TILES + k - 1))
                act.activation(th[0:rows, k % 2, :], up_banks[k % 2][0:rows, :], ACT.Tanh, scale=0.5).then_inc(s_tanh, 1)

            def y_high(b):
                act.wait_ge(s_yrstd, b + 1)
                act.wait_ge(s_yv, b + 1)
                for t in range(T):
                    ins = act.activation(y_split[:, 0, t, :], yv[:, t, :], ACT.Copy, scale=y_rstd[:, t:t + 1])
                ins.then_inc(s_yhigh, 1)

            def start():
                for name in PREP_USES:
                    if name == "stack0":
                        high_parts(0)
                    misc_use(name, Uses(None, True), None, 0)

            def run(att, ffn, prep, end, slots):
                uses = uses_of(att, prep, slots)
                s_banks = score_banks(ffn)
                for s in slots:
                    if att is not None and s < UNITS:
                        exps(att, s, 0, s_banks)
                    if ffn is not None:
                        tanh(ffn, s)
                    if att is not None and s < UNITS:
                        exps(att, s, 1, s_banks)
                    if prep is not None and s == PREP_HIGH:
                        high_parts(prep)
                    if att is not None and s >= 4 and s % T == 0 and s // T <= G:
                        o_copy(att, s // T - 1, uses)
                    if att is not None and s == POST_Y:
                        y_high(att)
                    for name in MISC.get(s, ()):
                        if wanted(name, att, ffn, prep):
                            misc_use(name, uses, att, prep)
                    if ffn is not None and s == ROUTE:
                        act.wait_ge(s_gap, ffn + 1)
                        act.activation(e2[:, :], gap[:, :], ACT.Exp).then_inc(s_e2, 1)

            iterations(start, run, act)

        @block.vector
        def _(dve):
            v = dve
            for start in (s_act, s_hid, s_dn, s_comb, s_out, s_result):
                dve.sem_inc(start, CREDIT)
            c = Steps(dve, s_c, 0, 100)
            dve.wait_ge(s_small, 32)
            c.do(v.scalar_tensor_tensor(out=qks[:, :], in0=qs_sb[:, :], scalar=HD ** -0.5, in1=ks_sb[:, :],
                                        op0=ALU.mult, op1=ALU.mult))
            c.wait()
            c.do(v.tensor_scalar(qks_neg[:, :], qks[:, :], -1.0, None, ALU.mult))
            c.wait()
            c.do(v.tensor_tensor(squares[:, 0, 0:P], qks[:, :], qks_neg[:, :], ALU.max))
            c.wait()
            c.do(v.reduce_max(qks_max[:, :], squares[:, 0, 0:P], AX.X))
            c.wait()
            c.do(v.tensor_scalar(shift0[:, :], qks_max[:, :], -float(HD), SAFE, ALU.mult, ALU.add))
            c.wait()
            c.do(v.tensor_scalar(shift[:, :], shift0[:, :], 0.0, None, ALU.min))
            dve.wait_ge(s_ident, 1)
            v.tensor_copy(ident16[:, :], ident[:, :]).then_inc(s_ident16, 1)
            dve.wait_ge(s_const, 5)

            def split_weights(n):
                if n == 0:
                    dve.wait_ge(s_ffn_w, 48)
                    c.do(v.tensor_copy(gw_hi[:, :], gw[:, :]))
                    c.wait()
                    c.do(v.tensor_tensor(gw_lo[:, :], gw[:, :], gw_hi[:, :], ALU.subtract))
                v.tensor_copy(w_hi[:, n, :], w_raw[:, n, :]).then_inc(s_split, 1)
                dve.wait_ge(s_split, 2 * n + 1)
                v.tensor_tensor(w_lo[:, n, :], w_raw[:, n, :], w_hi[:, n, :], ALU.subtract).then_inc(s_split, 1)

            def moments_of(st, src, s_mom, mom, var, ready):
                for t in range(T):
                    st.do(v.bn_stats(s_mom[:, t, :], src(t)))
                st.wait()
                st.do(v.tensor_copy(held_dve[:, :], half[:, 0:1]))
                for t in range(T):
                    st.do(v.bn_aggr(mom[:, t, :], s_mom[:, t, :]))
                st.wait()
                v.tensor_scalar(var[:, :], mom[:, :, 1], LN_EPS, None, ALU.add).then_inc(ready, 1)

            def normalised(st, dst, src, mom, r):
                for t in range(T):
                    st.do(v.tensor_scalar(dst(t), src(t), mom[:, t, 0:1], r[:, t:t + 1],
                                          ALU.subtract, ALU.mult))

            def prep_ln(b):
                st = Steps(dve, s_prep, b, PREP_STEPS)
                dve.wait_ge(s_x if some(b) else s_x0, 16)
                moments_of(st, lambda t: tile_of(stream, b, t), stats, moments, var_eps, s_var)
                return st

            def prep_xn(b, st):
                dve.wait_ge(s_rstd, b + 1)
                for t in range(T):
                    ins = v.tensor_scalar(xn[:, t, :], tile_of(stream, b, t), moments[:, t, 0:1],
                                          rstd[:, t:t + 1], ALU.subtract, ALU.mult)
                    if t < T - 1:
                        st.do(ins)
                st.wait()
                ins.then_inc(s_xn, 1)

            def prep_squares(b, st, uses):
                dve.wait_ge(s_free, uses["qkv3"] + 1)
                st.do(v.tensor_tensor(squares[:, :, :], qkv[:, :, 0:2 * C], qkv[:, :, 0:2 * C], ALU.mult))
                st.wait()
                st.do(v.reduce_sum(ssq[:, :], squares[:, :, :].rearrange("p t (h c) -> p (t h) c", c=HD), AX.X))
                st.wait()
                st.do(v.tensor_scalar(msq[:, :], ssq[:, :], 1.0 / HD, None, ALU.mult))
                st.wait()
                st.do(v.tensor_scalar(guess[:, 0, :], msq[:, :].bitcast(U32), 1, 0xFFFFFFFF,
                                      ALU.logical_shift_right, ALU.bitwise_xor))
                st.wait()
                st.do(v.tensor_copy(held_dve[:, :], half[:, 0:1]))
                st.do(v.tensor_tensor(guess[:, 1, :], guess[:, 0, :], magic[:, :], ALU.add))
                st.wait()

            def prep_norm(b, st):
                root = guess[:, 1, :].bitcast(F32)
                for n in range(3):
                    st.do(v.tensor_tensor(newton[:, 0, :], msq[:, :], root, ALU.mult))
                    st.wait()
                    st.do(v.scalar_tensor_tensor(out=newton[:, 1, :], in0=newton[:, 0, :], scalar=-0.5,
                                                 in1=root, op0=ALU.mult, op1=ALU.mult))
                    st.wait()
                    st.do(v.scalar_tensor_tensor(out=newton[:, 2 + n, :], in0=newton[:, 1, :], scalar=1.5,
                                                 in1=root, op0=ALU.add, op1=ALU.mult))
                    st.wait()
                    root = newton[:, 2 + n, :]
                st.do(v.tensor_tensor(rms[:, :], msq[:, :], root, ALU.mult))
                st.wait()
                st.do(v.tensor_scalar(rms_eps[:, :], rms[:, :], QK_EPS, None, ALU.add))
                st.wait()
                st.do(v.reciprocal(inv[:, :], rms_eps[:, :]))
                st.wait()
                by_head = inv[:, :].rearrange("p (t h a) -> p t h a", t=T, a=1)
                for dst, first, h0 in ((qn[:, :, :].rearrange("p (t h) c -> p t h c", t=T), 0, 0),
                                       (kn[:, :, :].rearrange("p t (h c) -> p t h c", c=HD), C, H)):
                    st.do(v.tensor_tensor(dst, qkv[:, :, first:first + C].rearrange("p t (h c) -> p t h c", c=HD),
                                          spread(by_head[:, :, h0:h0 + H, :], 3, HD), ALU.mult))
                st.wait()
                v.tensor_tensor(kw[:, :, :].rearrange("p (t h) c -> p t (h c)", t=T), kn[:, :, :],
                                spread(qks[:, :].rearrange("p (a n) -> p a n", a=1), 1, T),
                                ALU.mult).then_inc(s_qkn, 1)

            def prep_low(b, st):
                dve.wait_ge(s_high, b + 1)
                q2 = spread(qn[:, :, :].rearrange("p n (a c) -> p n a c", a=1), 2, 2)
                k2 = spread(kw[:, :, :].rearrange("p n (a c) -> p n a c", a=1), 2, 2)
                q_hi, q_lo = stack[:, 0, :, 0, :, :], stack[:, 0, :, 1, :, :]
                k_hi, k_lo = stack[:, 1, :, :, 0, :], stack[:, 1, :, :, 1, :]
                st.do(v.tensor_tensor(q_lo, q2, q_hi, ALU.subtract))
                v.tensor_tensor(k_lo, k2, k_hi, ALU.subtract).then_inc(s_stack, 1)
                assert st.n == PREP_STEPS, st.n

            PREP_STEPS = (2 * T + 1) + (T - 1) + 6 + (3 * 3 + 2 + 1 + 2) + 1

            def o_norm(b, g, uses):
                dve.wait_ge(s_full, uses[f"oT{g}"] + 1)
                view = misc[:, :].rearrange("p (t j c) -> p t j c", t=T, c=32)
                v.reciprocal(recip[:, :, :], view[:, :, :, HD]).then_inc(s_attn, 1)
                dve.wait_ge(s_attn, b * G + g + 1)
                v.tensor_tensor(attn[:, :, 32 * g:32 * g + 32].rearrange("p t (j c) -> p t j c", c=HD),
                                view[:, :, :, 0:HD],
                                spread(recip[:, :, :].rearrange("p t (j a) -> p t j a", a=1), 3, HD),
                                ALU.mult).then_inc(s_free, 1)

            POST_STEPS = 2 * (2 * T + 1) + 3 * T
            ROUTE_STEPS = 1 + T + 1 + T + 1 + 4 + 2 * T + 1

            def post_z(b, uses):
                st = Steps(dve, s_post, b, POST_STEPS)
                dve.wait_ge(s_full, uses["proj"] + 1)
                v.tensor_tensor(z[:, :, :], misc[:, :].rearrange("p (t c) -> p t c", t=T),
                                spread(bproj_sb[:, :].rearrange("p (a c) -> p a c", a=1), 1, T),
                                ALU.add).then_inc(s_free, 1)
                dve.wait_ge(s_free, uses["proj"] + 1)
                moments_of(st, lambda t: z[:, t, :], p_stats, p_moments, p_var, s_pvar)
                return st

            def post_x1(b, st):
                dve.wait_ge(s_prstd, 2 * b + 1)
                normalised(st, lambda t: zn[:, t, :], lambda t: z[:, t, :], p_moments, p_rstd)
                st.wait()
                for t in range(T):
                    st.do(v.tensor_tensor(x1[:, t, :], tile_of(stream, b, t), zn[:, t, :], ALU.add))
                st.wait()
                moments_of(st, lambda t: x1[:, t, :], p_stats, p_moments, p_var, s_pvar)

            def post_v(b, st):
                for t in range(T):
                    ins = v.scalar_tensor_tensor(out=yv[:, t, :], in0=x1[:, t, :],
                                                 scalar=p_moments[:, t, 0:1], in1=rms_sb[:, :],
                                                 op0=ALU.subtract, op1=ALU.mult)
                ins.then_inc(s_yv, 1)
                for t in range(T):
                    st.do(v.tensor_copy(tile_of(stream, b, t), x1[:, t, :]))
                assert st.n == POST_STEPS, st.n

            def post_y(b, st):
                dve.wait_ge(s_yhigh, b + 1)
                for t in range(T):
                    ins = v.scalar_tensor_tensor(out=y_split[:, 1, t, :], in0=yv[:, t, :],
                                                 scalar=y_rstd[:, t:t + 1], in1=y_split[:, 0, t, :],
                                                 op0=ALU.mult, op1=ALU.subtract)
                ins.then_inc(s_y, 1)

            def router(b, uses):
                st = Steps(dve, s_route, b, ROUTE_STEPS)
                dve.wait_ge(s_full, uses["logits"] + 1)
                v.tensor_copy(logit[:, :, :], misc[:, 0:T * E].rearrange("p (t e) -> p t e", t=T)
                              ).then_inc(s_free, 1)
                dve.wait_ge(s_free, uses["logits"] + 1)
                st.do(v.tensor_copy(held_dve[:, :], half[:, 0:1]))
                for t in range(T):
                    st.do(v.max(top[:, t, :], logit[:, t, :]))
                st.wait()
                v.tensor_tensor(gap[:, :], top[:, :, 1], top[:, :, 0], ALU.subtract).then_inc(s_gap, 1)
                st.do(v.tensor_copy(held_dve[:, :], half[:, 0:1]))
                for t in range(T):
                    st.do(v.max_index(top_at[:, t, :], top[:, t, :], logit[:, t, :]))
                st.wait()
                st.do(v.tensor_copy(top_no[:, :, :], top_at[:, :, 0:2]))
                for t in range(T):
                    v.tensor_scalar(xin[:, t, :], x1[:, t, :], p_moments[:, t, 0:1], p_rstd[:, t:t + 1],
                                    ALU.subtract, ALU.mult)
                dve.wait_ge(s_e2, b + 1)
                st.do(v.tensor_scalar(e_sum[:, :], e2[:, :], 1.0, None, ALU.add))
                st.wait()
                st.do(v.reciprocal(e_inv[:, :], e_sum[:, :]))
                st.wait()
                st.do(v.tensor_scalar(w_top[:, 0, :], e_inv[:, :], 0.5, None, ALU.mult))
                st.wait()
                st.do(v.tensor_tensor(w_top[:, 1, :], w_top[:, 0, :], e2[:, :], ALU.mult))
                st.wait()
                for n, dst in enumerate((w_a, w_b)):
                    for t in range(T):
                        st.do(v.tensor_scalar(dst[:, t, :], expert_no[:, :], top_no[:, t, n:n + 1],
                                              w_top[:, n, t:t + 1], ALU.is_equal, ALU.mult))
                st.wait()
                st.do(v.tensor_tensor(route[:, :], w_a[:, :, :].rearrange("p t e -> p (t e)"),
                                      w_b[:, :, :].rearrange("p t e -> p (t e)"), ALU.add))
                assert st.n == ROUTE_STEPS, st.n

            def hidden(b, k, banks):
                rows = PARTS[k % len(PARTS)][1]
                dve.wait_ge(s_tanh, b * TILES + k + 1)
                dve.wait_ge(s_hid, upto(b * TILES + k - 1))
                v.scalar_tensor_tensor(out=act2[0:rows, k % 2, :], in0=th[0:rows, k % 2, :], scalar=1.0,
                                       in1=up_banks[k % 2][0:rows, :], op0=ALU.add,
                                       op1=ALU.mult).then_inc(s_act, 1)
                dve.wait_ge(s_act, upto(b * TILES + k + 1))
                dve.wait_ge(s_gate, b * TILES + k + 1)
                dve.wait_ge(s_dn, upto(b * TILES + k + 1 - HR))
                v.tensor_tensor(hid[0:rows, k % HR, :], act2[0:rows, k % 2, :],
                                banks[k % len(banks)][0:rows, :], ALU.mult).then_inc(s_hid, 1)

            def combine(b, e, banks):
                dve.wait_ge(s_dn, upto(b * TILES + (e + 1) * len(PARTS)))
                if e == 0:
                    dve.wait_ge(s_route, (b + 1) * ROUTE_STEPS)
                    dve.wait_ge(s_result, upto(b))
                else:
                    dve.wait_ge(s_comb, upto(b * E + e))
                for t in range(T):
                    before = xin if e == 0 else acc
                    ins = v.scalar_tensor_tensor(out=acc[:, t, :],
                                                 in0=banks[e % len(banks)][:, t * C:(t + 1) * C],
                                                 scalar=route[:, t * E + e:t * E + e + 1],
                                                 in1=before[:, t, :], op0=ALU.mult, op1=ALU.add)
                ins.then_inc(s_comb, 1)

            FIN_STEPS = 2 * T + 1

            def final(b):
                dve.wait_ge(s_comb, upto((b + 1) * E))
                dve.wait_ge(s_result, upto(b))
                st = Steps(dve, s_fin, b, FIN_STEPS)
                moments_of(st, lambda t: acc[:, t, :], f_stats, f_moments, f_var, s_fvar)
                assert st.n == FIN_STEPS

            def start():
                st = prep_ln(0)
                prep_xn(0, st)
                prep_squares(0, st, Uses(None, True))
                prep_norm(0, st)
                prep_low(0, st)

            st_prep = st_post = None

            def run(att, ffn, prep, end, slots):
                nonlocal st_prep, st_post
                uses = uses_of(att, prep, slots)
                g_banks, d_banks = gate_banks(att), down_banks(att)
                for s in slots:
                    if end is not None and s == FINAL:
                        combine(end, E - 1, down_banks(0))
                        final(end)
                    if ffn is not None and s == ROUTE:
                        router(ffn, uses)
                    if ffn is not None and s >= 4 and (s - 4) % len(PARTS) == 0:
                        combine(ffn, (s - 4) // len(PARTS), d_banks)
                    if prep is not None:
                        if s == PREP_LN:
                            st_prep = prep_ln(prep)
                        elif s == PREP_XN:
                            prep_xn(prep, st_prep)
                        elif s == PREP_SQUARES:
                            prep_squares(prep, st_prep, uses)
                        elif s == PREP_NORM:
                            prep_norm(prep, st_prep)
                        elif s == PREP_LOW:
                            prep_low(prep, st_prep)
                    if ffn is not None:
                        hidden(ffn, s, g_banks)
                    elif s in (3, 6):
                        split_weights((s - 3) // 3)
                    if att is not None:
                        if s >= 5 and s % T == 1 and s // T <= G:
                            o_norm(att, s // T - 1, uses)
                        if s == POST_Z:
                            st_post = post_z(att, uses)
                        elif s == POST_X1:
                            post_x1(att, st_post)
                        elif s == POST_V:
                            post_v(att, st_post)
                        elif s == POST_Y:
                            post_y(att, st_post)

            iterations(start, run, dve)
            combine(B - 1, E - 1, down_banks(None))
            final(B - 1)


def kernel(L0_attn_x, L0_attn_Wqkv, L0_attn_Wproj, L0_attn_bproj, L0_attn_q_scale, L0_attn_k_scale,
           L0_ffn_gate_w, L0_ffn_rms_w, L0_ffn_W1, L0_ffn_W2, L0_ffn_W3):
    import numpy as np
    import concourse.bacc as bacc
    from concourse.bass_utils import run_bass_kernel_spmd

    def rows(a, repeat=1):
        return np.ascontiguousarray(np.broadcast_to(np.tile(np.asarray(a), repeat), (P, a.shape[0] * repeat)))

    arrays = {
        "x": np.ascontiguousarray(L0_attn_x),
        "wqkv": np.ascontiguousarray(L0_attn_Wqkv),
        "wproj": np.ascontiguousarray(L0_attn_Wproj),
        "bproj": rows(L0_attn_bproj),
        "q_scale": rows(L0_attn_q_scale, H),
        "k_scale": rows(L0_attn_k_scale, H),
        "gate_wT": np.ascontiguousarray(np.asarray(L0_ffn_gate_w).T),
        "rms_w": rows(L0_ffn_rms_w),
        "w1T": np.ascontiguousarray(np.asarray(L0_ffn_W1).reshape(E * DE, C).T),
        "w2T": np.ascontiguousarray(np.asarray(L0_ffn_W2).reshape(E * DE, C).T),
        "w3T": np.ascontiguousarray(np.asarray(L0_ffn_W3).transpose(0, 2, 1)),
    }
    nc = bacc.Bacc("TRN2", target_bir_lowering=False, num_devices=1)
    args = [nc.dram_tensor(f"in_{name}", a.shape, mybir.dt.from_np(a.dtype), kind="ExternalInput").ap()
            for name, a in arrays.items()]
    out = nc.dram_tensor("out_dram", (B, N, C), F32, kind="ExternalOutput").ap()
    layers(nc, *args, out)
    r = run_bass_kernel_spmd(nc, [{f"in_{name}": a for name, a in arrays.items()}], core_ids=[0])
    return r.results[0]["out_dram"]
```

```python
import concourse.bass as bass
from concourse import mybir
from contextlib import ExitStack

F32 = mybir.dt.float32
F16 = mybir.dt.float16
U32 = mybir.dt.uint32
ALU = mybir.AluOpType
ACT = mybir.ActivationFunctionType
AX = mybir.AxisListType

P = 128
B, N, C = 4, 512, 128
T = N // P
H, HD = 16, 8
G = H // 4
E, DE = 8, 352
PARTS = [(0, 128), (128, 128), (256, 96)]
TILES = E * len(PARTS)
UNITS = G * T
SLOTS = TILES
SAFE = 60.0
MAGIC = 0x5F3759DF
LN_EPS, QK_EPS, FFN_EPS = 1e-5, 1e-8, 1e-6

SPAN = 16


def slot_of(unit):
    return unit * SPAN // UNITS


UNITS_OF = [[u for u in range(UNITS) if slot_of(u) == s] for s in range(SLOTS)]
GROUP_END = {slot_of(T * (g + 1)): g for g in range(G)}
GROUP_NORM = {s + 1: g for s, g in GROUP_END.items()}

MISC = {0: ["logits"], 5: ["xT"], 6: ["qkv0", "qkv1"], 7: ["qkv2", "qkv3"],
        SPAN + 1: ["aT"], SPAN + 2: ["proj"], SPAN + 3: ["stack0"], SPAN + 4: ["stack1", "stack2"],
        SPAN + 5: ["stack3"], SPAN + 7: ["yT"]}
for s, g in GROUP_NORM.items():
    MISC[s] = [f"oT{g}"] + MISC.get(s, [])
PREP_LN, PREP_XN, PREP_SQUARES, PREP_GUESS, PREP_ROOT, PREP_INV, PREP_NORM, PREP_LOW = (
    2, 4, 8, 9, 11, 12, 15, 17)
PREP_V = [SPAN + 1, SPAN + 2]
POST_Z, POST_X1, POST_MOMENTS, POST_V, POST_Y = (SPAN + n for n in (2, 3, 4, 5, 6))
TOP2, RESIDUAL, ROUTE = 2, 0, 4
SPLIT = [5, 7]


def final_slots(att):
    return (0, 0, 0, 1) if att is not None else (1, 1, 6, 8)


WARM_FOR_X, WARM_FOR_QK, WARM_FOR_PROBS, WARM_FOR_Y = 4, 1, 1, 4
LAG = 2
CUT = 2

PREP_USES = ["xT", "qkv0", "qkv1", "qkv2", "qkv3"]
STACKS = [f"stack{t}" for t in range(T)]
ALL_USES = [name for slot in sorted(MISC) for name in MISC[slot] if name not in STACKS]
POST_USES = [name for name in ALL_USES if name not in PREP_USES]
N_PREP, N_ALL = len(PREP_USES), len(ALL_USES)
assert ALL_USES[0] == "logits"

START_DVE = (1, 3)

CREDIT = 4


def upto(n):
    return n + CREDIT


def spread(ap, axis, n):
    shape = list(ap.shape)
    shape[axis] = n
    return ap.broadcast_to(shape)


class Uses:

    def __init__(self, b, prep):
        self.b, self.alone = b, b is None
        self.base = 0 if b is None else b * N_ALL + N_PREP - 1
        self.names = PREP_USES if b is None else ALL_USES if prep else POST_USES

    def __getitem__(self, name):
        if isinstance(self.b, int) and self.b == B:
            return self.base - N_PREP + self.names.index(name)
        return self.base + self.names.index(name)


class Steps:

    def __init__(self, eng, sem, b, per, done=0):
        self.eng, self.sem, self.b, self.per, self.n = eng, sem, b, per, done

    def do(self, instruction):
        self.n += 1
        assert self.n <= self.per
        instruction.then_inc(self.sem, 1)

    def wait(self):
        self.eng.wait_ge(self.sem, self.b * self.per + self.n)


def layers(nc, x, wqkv, wproj, bproj, q_scale, k_scale, gate_wT, rms_w, w1T, w2T, w3T, out):
    with ExitStack() as ctx:
        def sb(name, shape, dt=F32):
            return ctx.enter_context(nc.sbuf_tensor(name, shape, dt))

        def sem(name):
            return ctx.enter_context(nc.semaphore(name))

        stream = sb("stream", [P, B * T, C])
        wqkv_sb = sb("wqkv_sb", [P, 3 * C])
        wproj_sb = sb("wproj_sb", [P, C])
        bproj_sb = sb("bproj_sb", [P, C])
        proj_sums = sb("proj_sums", [P, 2])
        proj_means = sb("proj_means", [P, 2])
        wproj_c = sb("wproj_c", [P, C])
        bproj_c = sb("bproj_c", [P, C])
        bproj_hi = sb("bproj_hi", [P, T, C], F16)
        bproj_lo = sb("bproj_lo", [P, T, C], F16)
        share = sb("share", [P, P], F16)
        rms_sb = sb("rms_sb", [P, C])
        qs_sb = sb("qs_sb", [P, H * HD])
        ks_sb = sb("ks_sb", [P, H * HD])
        qks = sb("qks", [P, H * HD])
        w_raw = sb("w_raw", [P, 2, E * DE])
        w_hi = sb("w_hi", [P, 2, E * DE], F16)
        w_lo = sb("w_lo", [P, 2, E * DE], F16)
        w3_raw = sb("w3_raw", [P, E, len(PARTS), C])
        w3_hi = sb("w3_hi", [P, E, len(PARTS), C], F16)
        w3_lo = sb("w3_lo", [P, E, len(PARTS), C], F16)
        gw = sb("gw", [P, E])
        gw_hi = sb("gw_hi", [P, E], F16)
        gw_lo = sb("gw_lo", [P, E], F16)
        ident = sb("ident", [P, P])
        ident16 = sb("ident16", [P, P], F16)
        expert_no = sb("expert_no", [P, E])
        half = sb("half", [P, 1])
        magic = sb("magic", [P, T * 2 * H], U32)
        neg_half = sb("neg_half", [P, T])
        qks_neg = sb("qks_neg", [P, H * HD])
        qks_abs = sb("qks_abs", [P, H * HD])
        qks_max = sb("qks_max", [P, 1])
        shift0 = sb("shift0", [P, 1])
        shift = sb("shift", [P, 1])
        held_dve = sb("held_dve", [P, 1])
        warm = sb("warm", [P, 1])
        held_pool = sb("held_pool", [P, T])

        stats = sb("stats", [P, T, 6])
        moments = sb("moments", [P, T, 2])
        var_eps = sb("var_eps", [P, T])
        rstd = sb("rstd", [P, T])
        xn = sb("xn", [P, T, C])
        xnT = sb("xnT", [P, N])
        qkv = sb("qkv", [P, T, 3 * C])
        squares = sb("squares", [P, T, 2 * C])
        ssq = sb("ssq", [P, T * 2 * H])
        msq = sb("msq", [P, T * 2 * H])
        guess = sb("guess", [P, 2, T * 2 * H], U32)
        newton = sb("newton", [P, 5, T * 2 * H])
        rms = sb("rms", [P, T * 2 * H])
        rms_eps = sb("rms_eps", [P, T * 2 * H])
        inv = sb("inv", [P, T * 2 * H])
        qn = sb("qn", [P, T * H, HD])
        kn = sb("kn", [P, T, H * HD])
        kw = sb("kw", [P, T * H, HD])
        stack = sb("stack", [P, 2, T * H, 2, 2, HD], F16)
        qkT = sb("qkT", [P, 2 * G, N], F16)
        v_ext = sb("v_ext", [P, T * H, 32])

        PR = 8
        probs = sb("probs", [P, PR, N])
        oT = sb("oT", [P, N])
        recip = sb("recip", [P, T, 4])
        attn = sb("attn", [P, T, C])
        attnT = sb("attnT", [P, N])
        p_stats = sb("p_stats", [P, T, 6])
        p_moments = sb("p_moments", [P, T, 2])
        p_var = sb("p_var", [P, T])
        p_rstd = sb("p_rstd", [P, T])
        xin = sb("xin", [P, T, C])
        y_var = sb("y_var", [P, T])
        y_rstd = sb("y_rstd", [P, T])
        yv = sb("yv", [P, T, C])
        y_split = sb("y_split", [P, 2, T, C], F16)
        yT = sb("yT", [P, B, 2 * N], F16)
        logit = sb("logit", [P, T, E])
        top = sb("top", [P, T, E])
        top_at = sb("top_at", [P, T, E], U32)
        top_no = sb("top_no", [P, T, 2])
        gap = sb("gap", [P, T])
        e2 = sb("e2", [P, T])
        e_sum = sb("e_sum", [P, T])
        e_inv = sb("e_inv", [P, T])
        w_top = sb("w_top", [P, 2, T])
        w_a = sb("w_a", [P, T, E])
        w_b = sb("w_b", [P, T, E])
        route = sb("route", [P, T * E])

        th = sb("th", [P, 2, N])
        act2 = sb("act2", [P, 2, N])
        HR = 4
        hid = sb("hid", [P, HR, N])
        hid_hi = sb("hid_hi", [P, HR, N], F16)
        hid_lo = sb("hid_lo", [P, HR, N], F16)
        acc = sb("acc", [P, T, C])
        acc_last = sb("acc_last", [P, T, C])
        f_stats = sb("f_stats", [P, T, 6])
        f_moments = sb("f_moments", [P, T, 2])
        f_var = sb("f_var", [P, T])
        f_rstd = sb("f_rstd", [P, T])
        fn = sb("fn", [P, T, C])
        result = sb("result", [P, T, C])

        def banks_of(name, n):
            return ctx.enter_context(nc.psum_tensor(name, [P, n, N], F32))

        groups = [banks_of("bank01", 2), banks_of("bank2", 1), banks_of("bank34", 2)] + [
            banks_of(f"bank{i}", 1) for i in (5, 6, 7)]
        bank = [group[:, i, :] for group in groups for i in range(group.shape[1])]
        o_bank, misc = bank[2], bank[7]
        def score_banks(ffn):
            return bank[0:2] if ffn is not None else bank[0:2] + bank[3:5]

        up_banks = bank[3:5]

        def gate_banks(att):
            return bank[5:6] if att is not None else [bank[5], bank[0]]

        def down_banks(att):
            return bank[6:7] if att is not None else [bank[6], bank[1]]

        s_wqkv = sem("wqkv_in")
        s_x0, s_x, s_small, s_attn_w, s_ffn_w, s_w3 = (
            sem(n) for n in ("x0_in", "x_in", "small_in", "attn_w_in", "ffn_w_in", "w3_in"))
        s_id0, s_ident, s_ident16, s_const, s_vzero = (
            sem(n) for n in ("ident_zero", "ident", "ident16", "constants", "v_zero"))
        s_c = sem("constant_steps")
        s_split, s_w3_split, s_centred = sem("weights_split"), sem("w3_split"), sem("projection_centred")
        s_full, s_free = sem("misc_full"), sem("misc_free")
        s_qkt_full, s_qkt_free = sem("qkT_full"), sem("qkT_free")
        s_prep = sem("prep_steps")
        s_var, s_rstd = sem("prep_var"), sem("prep_rstd")
        s_xn = sem("xn_ready")
        s_qkn, s_high = sem("qk_normed"), sem("high_parts")
        s_stack, s_v = sem("stack_ready"), sem("v_ready")
        s_qk, s_exp, s_pv, s_o, s_attn = (
            sem(n) for n in ("scores_done", "probs_done", "pv_done", "o_copied", "attn_steps"))
        s_post, s_pvar, s_prstd, s_y = (
            sem(n) for n in ("post_steps", "post_var", "post_rstd", "y_ready"))
        s_gap, s_e2 = sem("gap_ready"), sem("e2_ready")
        s_up, s_gate, s_tanh, s_act, s_hid, s_dn, s_comb = (
            sem(n) for n in ("up_done", "gate_done", "tanh_done", "act_done", "hid_done", "down_done", "combined"))
        s_route, s_yv, s_yrstd, s_yhigh = sem("route_steps"), sem("yv_ready"), sem("y_rstd"), sem("y_high")
        s_hi_dve, s_hi_act, s_lo = sem("hid_high_dve"), sem("hid_high_act"), sem("hid_low")
        s_fin, s_fvar, s_frstd, s_result, s_out = (
            sem(n) for n in ("final_steps", "final_var", "final_rstd", "result_ready", "out_written"))

        block = ctx.enter_context(nc.Block())

        def misc_bank(name, att):
            if name in STACKS:
                t = int(name[-1])
                return bank[4 + t] if att is None else bank[t % 2]
            if att is None and name.startswith("qkv"):
                return bank[int(name[-1])]
            return misc

        def uses_of(att, prep):
            return Uses(B, True) if att is None else Uses(att, prep is not None)

        def high_on_dve(k, att):
            return att is not None and k < SPAN

        def wait_for_high(eng, b, k, att):
            if high_on_dve(k, att):
                eng.wait_ge(s_hi_dve, b * SPAN + k + 1)
            else:
                eng.wait_ge(s_hi_act, b * (TILES - SPAN) + (k if att is None else k - SPAN) + 1)

        def wanted(name, att, ffn, prep):
            stage = ffn if name == "logits" else prep if name in PREP_USES + STACKS else att
            return stage is not None

        def early_and_late(s, att, ffn, prep):
            names = [n for n in MISC.get(s, ()) if wanted(n, att, ffn, prep)]
            n_late = 1 if names and (ffn is None or names[-1][0] not in "oy") else 0
            return names[:len(names) - n_late], names[len(names) - n_late:]

        def tile_of(ap, b, t):
            if isinstance(b, int):
                return ap[:, b * T + t, :]
            return ap[:, bass.ds(b * T + t, 1), :].rearrange("p a c -> p (a c)")

        def batch_of(ap, b):
            if isinstance(b, int):
                return ap[:, b, :]
            return ap[:, bass.ds(b, 1), :].rearrange("p a n -> p (a n)")

        def some(b):
            return not isinstance(b, int) or b > 0

        def iterations(start, run, eng):
            start()
            run(0, None, 1, None, range(SLOTS))
            run(1, 0, 2, None, range(CUT))
            with eng.Fori(1, B - 1) as b:
                run(b, b - 1, b + 1, None, range(CUT, SLOTS))
                run(b + 1, b, None, b - 1, range(CUT))
            run(B - 1, B - 2, None, None, range(CUT, SLOTS))
            run(None, B - 1, None, B - 2, range(SLOTS))

        @block.sync
        def _(sp):
            rows = x.rearrange("b (t p) c -> p (b t) c", p=P)
            sp.dma_start(stream[:, 0:T, :], rows[:, 0:T, :]).then_inc(s_x0, 16)
            sp.dma_start(wqkv_sb[:, :], wqkv).then_inc(s_wqkv, 16)
            sp.dma_start(qs_sb[:, :], q_scale).then_inc(s_small, 16)
            sp.dma_start(ks_sb[:, :], k_scale).then_inc(s_small, 16)
            sp.dma_start(stream[:, T:B * T, :], rows[:, T:B * T, :]).then_inc(s_x, 16)
            sp.dma_start(wproj_sb[:, :], wproj).then_inc(s_attn_w, 16)
            sp.dma_start(bproj_sb[:, :], bproj).then_inc(s_attn_w, 16)
            sp.dma_start(rms_sb[:, :], rms_w).then_inc(s_attn_w, 16)
            sp.dma_start(gw[:, :], gate_wT).then_inc(s_ffn_w, 16)
            sp.dma_start(w_raw[:, 0, :], w1T).then_inc(s_ffn_w, 16)
            sp.dma_start(w_raw[:, 1, :], w2T).then_inc(s_ffn_w, 16)
            for i, (first, rows_i) in enumerate(PARTS):
                sp.dma_start(w3_raw[0:rows_i, :, i, :],
                             w3T[:, first:first + rows_i, :].rearrange("e p m -> p e m")).then_inc(s_w3, 16)

            def store(b):
                sp.wait_ge(s_result, upto(b + 1))
                dst = out[b] if isinstance(b, int) else out[bass.ds(b, 1)].rearrange("a n c -> (a n) c")
                sp.dma_start(dst.rearrange("(t p) c -> p t c", p=P), result[:, :, :]).then_inc(s_out, 16)

            def run(att, ffn, prep, end, slots):
                if end is not None:
                    store(end)

            iterations(lambda: None, run, sp)
            store(B - 1)
            sp.wait_ge(s_out, upto(16 * B))

        @block.gpsimd
        def _(pool):
            pool.memset(ident[:, :], 0.0).then_inc(s_id0, 1)
            pool.memset(neg_half[:, :], -0.5).then_inc(s_const, 1)
            pool.memset(half[:, :], 0.5).then_inc(s_const, 1)
            pool.memset(share[:, :], 1.0 / P).then_inc(s_const, 1)
            pool.memset(magic[:, :], MAGIC + 1).then_inc(s_const, 1)
            pool.wait_ge(s_id0, 1)
            pool.affine_select(out=ident[:, :], in_=ident[:, :], compare_op=ALU.not_equal, fill=1.0,
                               base=0, pattern=[[-1, P]], channel_multiplier=1).then_inc(s_ident, 1)
            pool.iota(expert_no[:, :], [[1, E]], base=0, channel_multiplier=0,
                      allow_small_or_imprecise_dtypes=True).then_inc(s_const, 1)
            pool.memset(v_ext[:, :, :], 0.0).then_inc(s_vzero, 1)
            pool.wait_ge(s_vzero, 1)
            pool.memset(v_ext[:, :, HD:HD + 1], 1.0).then_inc(s_vzero, 1)
            pool.wait_ge(s_vzero, 2)
            pool.wait_ge(s_const, 5)

            def norm_power(b, ready, done, src, dst, n, of):
                pool.wait_ge(ready, b * of + n + 1)
                pool.tensor_tensor(dst[:, :], src[:, :], neg_half[:, :], ALU.pow).then_inc(done, 1)

            def prep_v(b, uses, tiles):
                if some(b):
                    pool.wait_ge(s_pv, b * UNITS)
                pool.wait_ge(s_free, uses["qkv3"] + 1)
                held = held_pool[:, tiles[0]:tiles[0] + 1]
                pool.tensor_tensor(held, half[:, 0:1], half[:, 0:1], ALU.mult)
                for t in tiles:
                    ins = pool.tensor_copy(v_ext[:, t * H:(t + 1) * H, 0:HD],
                                           qkv[:, t, 2 * C:3 * C].rearrange("p (h c) -> p h c", c=HD))
                if T - 1 in tiles:
                    ins.then_inc(s_v, 1)

            def hidden_low(b, k, att):
                rows = PARTS[k % len(PARTS)][1]
                wait_for_high(pool, b, k, att)
                pool.tensor_tensor(hid_lo[0:rows, k % HR, :], hid[0:rows, k % HR, :],
                                   hid_hi[0:rows, k % HR, :], ALU.subtract).then_inc(s_lo, 1)

            def post_z(b):
                norm_power(b, s_pvar, s_prstd, p_var, p_rstd, 0, 2)

            def post_x1(b):
                pool.wait_ge(s_pvar, b * 2 + 2)
                pool.tensor_tensor(y_rstd[:, :], y_var[:, :], neg_half[:, :], ALU.pow).then_inc(s_yrstd, 1)
                norm_power(b, s_pvar, s_prstd, p_var, p_rstd, 1, 2)

            def split_w3():
                pool.wait_ge(s_w3, 48)
                parts = ((slice(0, P), slice(0, 2)), (slice(0, PARTS[2][1]), slice(2, 3)))
                for rows, part in parts:
                    pool.tensor_copy(w3_hi[rows, :, part, :], w3_raw[rows, :, part, :]).then_inc(s_w3_split, 1)
                pool.wait_ge(s_w3_split, 2)
                for rows, part in parts:
                    pool.tensor_tensor(w3_lo[rows, :, part, :], w3_raw[rows, :, part, :],
                                       w3_hi[rows, :, part, :], ALU.subtract).then_inc(s_w3_split, 1)

            def start():
                norm_power(0, s_var, s_rstd, var_eps, rstd, 0, 1)
                prep_v(0, Uses(None, True), range(T))

            first_half, second_half = range(T // 2), range(T // 2, T)

            def run(att, ffn, prep, end, slots):
                for s in slots:
                    if ffn is not None and s >= 1:
                        hidden_low(ffn, s - 1, att)
                    if end is not None and s == 0:
                        hidden_low(end, SLOTS - 1, 0)
                    if end is not None and s == final_slots(att)[2]:
                        norm_power(end, s_fvar, s_frstd, f_var, f_rstd, 0, 1)
                    if prep is not None and s == PREP_LN:
                        norm_power(prep, s_var, s_rstd, var_eps, rstd, 0, 1)
                        if ffn is None:
                            split_w3()
                    if prep is not None and s in PREP_V:
                        prep_v(prep, Uses(att, True), (first_half, second_half)[PREP_V.index(s)])
                    if att is not None and s == POST_Z + 1:
                        post_z(att)
                    if att is not None and s == POST_MOMENTS + 1:
                        post_x1(att)

            iterations(start, run, pool)
            hidden_low(B - 1, SLOTS - 1, None)
            norm_power(B - 1, s_fvar, s_frstd, f_var, f_rstd, 0, 1)

        @block.tensor
        def _(pe):
            pe.wait_ge(s_ident, 1)

            def keep_warm(rounds, dst):
                with pe.Fori(0, rounds):
                    for _ in range(8):
                        pe.transpose(dst[:, 0:P], ident[:, :], ident[:, :])

            keep_warm(WARM_FOR_X, bank[6])
            pe.wait_ge(s_wqkv, 16)
            pe.wait_ge(s_ident16, 1)

            def fill(uses, name):
                n = uses[name]
                if uses.alone:
                    n = min(n, 1)
                if not isinstance(n, int) or n > 0:
                    pe.wait_ge(s_free, n)

            def transposes(dst, src, what):
                for t in range(T):
                    ins = pe.transpose(dst[:, t * P:(t + 1) * P], src(t), what[:, :])
                return ins

            def misc_use(name, uses, att, prep, y_ffn=None):
                misc = misc_bank(name, att)
                misc16 = misc[:, :].bitcast(F16)
                if name == "xT":
                    pe.wait_ge(s_xn, prep + 1)
                    fill(uses, name)
                    ins = transposes(misc, lambda t: xn[:, t, :], ident)
                elif name.startswith("qkv"):
                    t = int(name[3:])
                    fill(uses, name)
                    ins = pe.matmul(misc[:, 0:3 * C], xnT[:, t * P:(t + 1) * P], wqkv_sb[:, :],
                                    start=True, stop=True)
                elif name.startswith("stack"):
                    t = int(name[5:])
                    pe.wait_ge(s_stack, prep + 1)
                    if not uses.alone and t >= 2:
                        pe.wait_ge(s_qkt_free, prep * T + t - 1)
                    for qk in range(2):
                        for g in range(G):
                            at = (qk * G + g) * P
                            src = stack[:, qk, t * H + 4 * g:t * H + 4 * g + 4, :, :, :]
                            ins = pe.transpose(misc16[:, at:at + P],
                                               src.rearrange("p h a b c -> p (h a b c)"), ident16[:, :])
                    ins.then_inc(s_qkt_full, 1)
                    return
                elif name.startswith("oT"):
                    g = int(name[2:])
                    pe.wait_ge(s_o, att * G + g + 1)
                    fill(uses, name)
                    ins = transposes(misc, lambda t: oT[:, t * P:(t + 1) * P], ident)
                elif name == "aT":
                    fill(uses, name)
                    pe.wait_ge(s_free, uses["oT3"] + 1)
                    ins = transposes(misc, lambda t: attn[:, t, :], ident)
                elif name == "proj":
                    fill(uses, name)
                    pe.wait_ge(s_free, uses["aT"] + 1)
                    for n, bias in enumerate((bproj_hi, bproj_lo)):
                        pe.matmul(misc[:, :], share[:, :], bias[:, :, :].rearrange("p t c -> p (t c)"),
                                  start=n == 0, stop=False, skip_group_check=True)
                    for t in range(T):
                        ins = pe.matmul(misc[:, t * C:(t + 1) * C], attnT[:, t * P:(t + 1) * P],
                                        wproj_c[:, :], start=False, stop=True, skip_group_check=True)
                elif name == "yT":
                    pe.wait_ge(s_y, att + 1)
                    fill(uses, name)
                    for s in range(2):
                        for t in range(T):
                            at = s * N + t * P
                            ins = pe.transpose(misc16[:, at:at + P], y_split[:, s, t, :], ident16[:, :])
                elif name == "logits":
                    fill(uses, name)
                    for t in range(T):
                        for i, (s, w) in enumerate(((0, gw_hi), (0, gw_lo), (1, gw_hi), (1, gw_lo))):
                            at = s * N + t * P
                            ins = pe.matmul(misc[:, t * E:(t + 1) * E], y_ffn[:, at:at + P], w[:, :],
                                            start=i == 0, stop=i == 3)
                ins.then_inc(s_full, 1)

            def scores(b, u, pair, banks):
                g, m = divmod(u, T)
                for j in (2 * pair, 2 * pair + 1):
                    n = 4 * u + j
                    if n >= len(banks):
                        pe.wait_ge(s_exp, b * 4 * UNITS + n - len(banks) + 1)
                    elif some(b):
                        pe.wait_ge(s_exp, b * 4 * UNITS)
                    r = slice(32 * j, 32 * j + 32)
                    pe.matmul(banks[n % len(banks)][:, :], qkT[r, G + g, m * P:(m + 1) * P], qkT[r, g, :],
                              start=True, stop=True).then_inc(s_qk, 1)

            def weighted(b, u):
                g, m = divmod(u, T)
                pe.wait_ge(s_exp, b * 4 * UNITS + 4 * u + 4)
                if u == 0:
                    pe.wait_ge(s_v, b + 1)
                if m == 0 and (g > 0 or some(b)):
                    pe.wait_ge(s_o, b * G + g)
                for j in range(4):
                    ins = pe.matmul(o_bank[32 * j:32 * j + 32, :], v_ext[:, m * H + 4 * g + j, :],
                                    probs[:, (4 * u + j) % PR, :], start=m == 0, stop=m == T - 1,
                                    skip_group_check=True)
                ins.then_inc(s_pv, 1)

            def expand(b, k, which, y_b, banks):
                e, i = divmod(k, len(PARTS))
                at, rows = e * DE + PARTS[i][0], PARTS[i][1]
                dst, done, used = banks[k % len(banks)], (s_up, s_gate)[which], (s_act, s_hid)[which]
                before = k + 1 - len(banks) if which == 0 else max(k + 1 - len(banks), 0)
                pe.wait_ge(used, upto(b * TILES + before))
                hi, lo = (w[:, which, at:at + rows] for w in (w_hi, w_lo))
                pe.matmul(dst[0:rows, :], hi, y_b[:, 0:N], start=True, stop=False)
                pe.matmul(dst[0:rows, :], hi, y_b[:, N:2 * N], start=False, stop=False)
                pe.matmul(dst[0:rows, :], lo, y_b[:, 0:N], start=False, stop=True).then_inc(done, 1)

            def contract(b, k, banks):
                e, i = divmod(k, len(PARTS))
                rows = PARTS[i][1]
                pe.wait_ge(s_lo, upto(b * TILES + k + 1))
                if i == 0:
                    pe.wait_ge(s_comb, upto(b * E + max(e + 1 - len(banks), 0)))
                for t in range(T):
                    for n, (h, w) in enumerate(((hid_hi, w3_hi), (hid_hi, w3_lo), (hid_lo, w3_hi))):
                        ins = pe.matmul(banks[e % len(banks)][:, t * C:(t + 1) * C],
                                        h[0:rows, k % HR, t * P:(t + 1) * P], w[0:rows, e, i, :],
                                        start=i == 0 and t == 0 and n == 0,
                                        stop=i == len(PARTS) - 1 and n == 2, skip_group_check=True)
                ins.then_inc(s_dn, 1)

            def start():
                for name in PREP_USES + STACKS:
                    misc_use(name, Uses(None, True), None, 0)
                keep_warm(WARM_FOR_QK, bank[2])

            def run(att, ffn, prep, end, slots):
                uses = uses_of(att, prep)
                s_banks, g_banks, d_banks = score_banks(ffn), gate_banks(att), down_banks(att)
                if att is not None and 0 in slots:
                    pe.wait_ge(s_qkt_free, (att + 1) * T)
                y_ffn = None if ffn is None else batch_of(yT, ffn)
                if att is None:
                    pe.wait_ge(s_exp, B * 4 * UNITS)
                for s in slots:
                    units = UNITS_OF[s] if att is not None else []
                    early, late = early_and_late(s, att, ffn, prep)
                    if units:
                        scores(att, units[0], 0, s_banks)
                    if ffn is not None:
                        if s == 0:
                            pe.wait_ge(s_free, uses["logits"])
                        expand(ffn, s, 0, y_ffn, up_banks)
                    if ffn is None and late == ["yT"]:
                        keep_warm(WARM_FOR_Y, bank[6])
                    if end is not None and s == 0:
                        contract(end, SLOTS - 2, down_banks(0))
                    for name in early:
                        misc_use(name, uses, att, prep, y_ffn)
                    if ffn is not None:
                        expand(ffn, s, 1, y_ffn, g_banks)
                    if units:
                        scores(att, units[0], 1, s_banks)
                        if ffn is None and s < 1:
                            keep_warm(WARM_FOR_PROBS, bank[6])
                        if units[0] > 0:
                            weighted(att, units[0] - 1)
                    if units[1:]:
                        scores(att, units[1], 0, s_banks)
                    if ffn is not None and s >= LAG:
                        contract(ffn, s - LAG, d_banks)
                    elif end is not None and s == final_slots(att)[0]:
                        contract(end, SLOTS - 1, down_banks(0))
                    if units[1:]:
                        scores(att, units[1], 1, s_banks)
                        weighted(att, units[0])
                    if att is not None and s == SPAN:
                        weighted(att, UNITS - 1)
                    if ffn is None and s == SPAN + 1:
                        pe.wait_ge(s_split, 4)
                        pe.wait_ge(s_w3_split, 4)
                        pe.wait_ge(s_centred, 1)
                    for name in late:
                        misc_use(name, uses, att, prep, y_ffn)

            iterations(start, run, pe)
            for k in range(SLOTS - LAG, SLOTS):
                contract(B - 1, k, down_banks(None))

        @block.scalar
        def _(act):
            act.wait_ge(s_const, 5)
            act.activation(warm[:, :], half[:, 0:1], ACT.Exp)
            act.wait_ge(s_c, 6)

            def copy_out(uses, name, dst, src):
                act.wait_ge(s_full, uses[name] + 1)
                act.activation(dst, src, ACT.Copy).then_inc(s_free, 1)

            def misc_use(name, uses, att, prep):
                misc = misc_bank(name, att)
                misc16 = misc[:, :].bitcast(F16)
                if name == "xT":
                    copy_out(uses, name, xnT[:, :], misc[:, :])
                elif name.startswith("qkv"):
                    if name == "qkv0" and some(prep):
                        act.wait_ge(s_v, prep)
                    t = int(name[3:])
                    copy_out(uses, name, qkv[:, t, :], misc[:, 0:3 * C])
                elif name.startswith("stack"):
                    t = int(name[5:])
                    act.wait_ge(s_qkt_full, prep * T + t + 1)
                    act.activation(qkT[:, :, t * P:(t + 1) * P], misc16.rearrange("p (a n) -> p a n", n=P),
                                   ACT.Copy).then_inc(s_qkt_free, 1)
                elif name == "aT":
                    copy_out(uses, name, attnT[:, :], misc[:, :])
                elif name == "yT":
                    copy_out(uses, name, batch_of(yT, att), misc16)

            def high_parts(b):
                for n, (dst, src) in enumerate(((stack[:, 0, :, 0, :, :], qn), (stack[:, 1, :, :, 0, :], kw))):
                    act.wait_ge(s_qkn, 2 * b + n + 1)
                    act.activation(dst, spread(src[:, :, :].rearrange("p n (a c) -> p n a c", a=1), 2, 2),
                                   ACT.Copy).then_inc(s_high, 1)

            def o_copy(b, g, uses):
                act.wait_ge(s_pv, b * UNITS + (g + 1) * T)
                if g > 0:
                    act.wait_ge(s_full, uses[f"oT{g - 1}"] + 1)
                act.activation(oT[:, :], o_bank[:, :], ACT.Copy).then_inc(s_o, 1)

            def exps(b, u, pair, banks):
                if len(banks) == 4:
                    n = 4 * u + 2 * pair
                    act.wait_ge(s_qk, b * 4 * UNITS + n + 2)
                    if u >= 2:
                        act.wait_ge(s_pv, b * UNITS + u - 1)
                    act.activation(probs[:, n % PR:n % PR + 2, :], groups[2 * pair][:, :, :], ACT.Exp,
                                   bias=shift[:, :]).then_inc(s_exp, 2)
                    return
                for j in (2 * pair, 2 * pair + 1):
                    n = 4 * u + j
                    act.wait_ge(s_qk, b * 4 * UNITS + n + 1)
                    if u >= 2:
                        act.wait_ge(s_pv, b * UNITS + u - 1)
                    elif some(b):
                        act.wait_ge(s_pv, b * UNITS)
                    act.activation(probs[:, n % PR, :], banks[n % len(banks)][:, :], ACT.Exp,
                                   bias=shift[:, :]).then_inc(s_exp, 1)

            def tanh(b, k):
                rows = PARTS[k % len(PARTS)][1]
                act.wait_ge(s_up, b * TILES + k + 1)
                act.wait_ge(s_act, upto(b * TILES + k - 1))
                act.activation(th[0:rows, k % 2, :], up_banks[k % 2][0:rows, :], ACT.Tanh,
                               scale=0.5).then_inc(s_tanh, 1)

            def hidden_high(b, k, att):
                if high_on_dve(k, att):
                    return
                rows = PARTS[k % len(PARTS)][1]
                act.wait_ge(s_hid, upto(b * TILES + k + 1))
                act.wait_ge(s_dn, upto(b * TILES + k + 1 - HR))
                act.activation(hid_hi[0:rows, k % HR, :], hid[0:rows, k % HR, :], ACT.Copy).then_inc(s_hi_act, 1)

            def y_high(b):
                act.wait_ge(s_yrstd, b + 1)
                act.wait_ge(s_yv, b + 1)
                for t in range(T):
                    ins = act.activation(y_split[:, 0, t, :], yv[:, t, :], ACT.Copy, scale=y_rstd[:, t:t + 1])
                ins.then_inc(s_yhigh, 1)

            def start():
                for name in PREP_USES + STACKS:
                    if name == "stack0":
                        high_parts(0)
                    if name not in [f"stack{t}" for t in START_DVE]:
                        misc_use(name, Uses(None, True), None, 0)

            def run(att, ffn, prep, end, slots):
                uses = uses_of(att, prep)
                s_banks = score_banks(ffn)
                for s in slots:
                    units = UNITS_OF[s] if att is not None else []
                    if units:
                        exps(att, units[0], 0, s_banks)
                    if ffn is not None:
                        tanh(ffn, s)
                        if s >= 1:
                            hidden_high(ffn, s - 1, att)
                    if end is not None and s == 0:
                        hidden_high(end, SLOTS - 1, 0)
                    early, late = early_and_late(s, att, ffn, prep)
                    for name in early:
                        misc_use(name, uses, att, prep)
                    if units:
                        exps(att, units[0], 1, s_banks)
                    if att is not None and s in GROUP_END:
                        o_copy(att, GROUP_END[s], uses)
                    for u in units[1:]:
                        exps(att, u, 0, s_banks)
                        exps(att, u, 1, s_banks)
                    if prep is not None and s == PREP_LOW:
                        high_parts(prep)
                    if att is not None and s == POST_Y:
                        y_high(att)
                    if ffn is not None and s == TOP2 + 1:
                        act.wait_ge(s_gap, ffn + 1)
                        act.activation(e2[:, :], gap[:, :], ACT.Exp).then_inc(s_e2, 1)
                    for name in late:
                        misc_use(name, uses, att, prep)

            iterations(start, run, act)
            hidden_high(B - 1, SLOTS - 1, None)

        @block.vector
        def _(dve):
            v = dve
            for start in (s_act, s_hid, s_lo, s_dn, s_comb, s_out, s_result):
                dve.sem_inc(start, CREDIT)
            c = Steps(dve, s_c, 0, 100)

            def constants():
                dve.wait_ge(s_small, 32)
                c.do(v.scalar_tensor_tensor(out=qks[:, :], in0=qs_sb[:, :], scalar=HD ** -0.5,
                                            in1=ks_sb[:, :], op0=ALU.mult, op1=ALU.mult))
                c.wait()
                c.do(v.tensor_scalar(qks_neg[:, :], qks[:, :], -1.0, None, ALU.mult))
                c.wait()
                c.do(v.tensor_tensor(qks_abs[:, :], qks[:, :], qks_neg[:, :], ALU.max))
                c.wait()
                c.do(v.reduce_max(qks_max[:, :], qks_abs[:, :], AX.X))
                c.wait()
                c.do(v.tensor_scalar(shift0[:, :], qks_max[:, :], -float(HD), SAFE, ALU.mult, ALU.add))
                c.wait()
                c.do(v.tensor_scalar(shift[:, :], shift0[:, :], 0.0, None, ALU.min))
                dve.wait_ge(s_ident, 1)
                v.tensor_copy(ident16[:, :], ident[:, :]).then_inc(s_ident16, 1)

            def centre_projection():
                dve.wait_ge(s_attn_w, 48)
                for n, (src, dst) in enumerate(((wproj_sb, wproj_c), (bproj_sb, bproj_c))):
                    c.do(v.reduce_sum(proj_sums[:, n:n + 1], src[:, :], AX.X))
                    c.wait()
                    c.do(v.tensor_scalar(proj_means[:, n:n + 1], proj_sums[:, n:n + 1], 1.0 / C, None, ALU.mult))
                    c.wait()
                    c.do(v.tensor_scalar(dst[:, :], src[:, :], proj_means[:, n:n + 1], None, ALU.subtract))
                    c.wait()
                by_tile = spread(bproj_c[:, :].rearrange("p (a c) -> p a c", a=1), 1, T)
                c.do(v.tensor_copy(bproj_hi[:, :, :], by_tile))
                c.wait()
                v.tensor_tensor(bproj_lo[:, :, :], by_tile, bproj_hi[:, :, :], ALU.subtract).then_inc(s_centred, 1)

            def split_weights(n):
                if n == 0:
                    dve.wait_ge(s_ffn_w, 48)
                    c.do(v.tensor_copy(gw_hi[:, :], gw[:, :]))
                    c.wait()
                    c.do(v.tensor_tensor(gw_lo[:, :], gw[:, :], gw_hi[:, :], ALU.subtract))
                v.tensor_copy(w_hi[:, n, :], w_raw[:, n, :]).then_inc(s_split, 1)
                dve.wait_ge(s_split, 2 * n + 1)
                v.tensor_tensor(w_lo[:, n, :], w_raw[:, n, :], w_hi[:, n, :], ALU.subtract).then_inc(s_split, 1)

            def moments_of(st, src, s_mom, mom, var, ready, both=None):
                for t in range(T):
                    st.do(v.bn_stats(s_mom[:, t, :], src(t)))
                st.wait()
                st.do(v.tensor_copy(held_dve[:, :], half[:, 0:1]))
                for t in range(T):
                    st.do(v.bn_aggr(mom[:, t, :], s_mom[:, t, :]))
                st.wait()
                if both is not None:
                    st.do(v.tensor_scalar(both[:, :], mom[:, :, 1], 1.0 + FFN_EPS, LN_EPS * FFN_EPS,
                                          ALU.mult, ALU.add))
                v.tensor_scalar(var[:, :], mom[:, :, 1], LN_EPS, None, ALU.add).then_inc(ready, 1)

            def normalised(st, dst, src, mom, r):
                for t in range(T):
                    st.do(v.tensor_scalar(dst(t), src(t), mom[:, t, 0:1], r[:, t:t + 1],
                                          ALU.subtract, ALU.mult))

            def prep_ln(b):
                st = Steps(dve, s_prep, b, PREP_STEPS)
                dve.wait_ge(s_x if some(b) else s_x0, 16)
                moments_of(st, lambda t: tile_of(stream, b, t), stats, moments, var_eps, s_var)
                return st

            def prep_xn(b, st):
                dve.wait_ge(s_rstd, b + 1)
                for t in range(T):
                    ins = v.tensor_scalar(xn[:, t, :], tile_of(stream, b, t), moments[:, t, 0:1],
                                          rstd[:, t:t + 1], ALU.subtract, ALU.mult)
                    if t < T - 1:
                        st.do(ins)
                st.wait()
                ins.then_inc(s_xn, 1)

            def prep_squares(b, st, uses):
                def square(t):
                    st.do(v.tensor_tensor(squares[:, t, :], qkv[:, t, 0:2 * C], qkv[:, t, 0:2 * C], ALU.mult))

                def by_head(t):
                    st.do(v.reduce_sum(ssq[:, t * 2 * H:(t + 1) * 2 * H],
                                       squares[:, t, :].rearrange("p (h c) -> p h c", c=HD), AX.X))

                if uses.alone:
                    for t in range(T):
                        dve.wait_ge(s_free, uses[f"qkv{t}"] + 1)
                        square(t)
                        st.wait()
                        by_head(t)
                else:
                    dve.wait_ge(s_free, uses["qkv3"] + 1)
                    for t in range(T):
                        square(t)
                    st.wait()
                    for t in range(T):
                        by_head(t)
                st.wait()

            def prep_guess(b, st):
                st.do(v.tensor_scalar(msq[:, :], ssq[:, :], 1.0 / HD, None, ALU.mult))
                st.wait()
                st.do(v.tensor_scalar(guess[:, 0, :], msq[:, :].bitcast(U32), 1, 0xFFFFFFFF,
                                      ALU.logical_shift_right, ALU.bitwise_xor))
                st.wait()
                st.do(v.tensor_copy(held_dve[:, :], half[:, 0:1]))
                st.do(v.tensor_tensor(guess[:, 1, :], guess[:, 0, :], magic[:, :], ALU.add))
                st.wait()

            def prep_root(b, st, n):
                root = newton[:, 1 + n, :] if n else guess[:, 1, :].bitcast(F32)
                st.do(v.tensor_tensor(newton[:, 0, :], msq[:, :], root, ALU.mult))
                st.wait()
                st.do(v.scalar_tensor_tensor(out=newton[:, 1, :], in0=newton[:, 0, :], scalar=-0.5,
                                             in1=root, op0=ALU.mult, op1=ALU.mult))
                st.wait()
                st.do(v.scalar_tensor_tensor(out=newton[:, 2 + n, :], in0=newton[:, 1, :], scalar=1.5,
                                             in1=root, op0=ALU.add, op1=ALU.mult))
                st.wait()

            def prep_inv(b, st):
                st.do(v.tensor_tensor(rms[:, :], msq[:, :], newton[:, 4, :], ALU.mult))
                st.wait()
                st.do(v.tensor_scalar(rms_eps[:, :], rms[:, :], QK_EPS, None, ALU.add))
                st.wait()
                st.do(v.reciprocal(inv[:, :], rms_eps[:, :]))
                st.wait()

            def prep_norm(b, st):
                by_head = inv[:, :].rearrange("p (t h a) -> p t h a", t=T, a=1)
                def by_rms(dst, first, h0):
                    return v.tensor_tensor(
                        dst, qkv[:, :, first:first + C].rearrange("p t (h c) -> p t h c", c=HD),
                        spread(by_head[:, :, h0:h0 + H, :], 3, HD), ALU.mult)

                by_rms(qn[:, :, :].rearrange("p (t h) c -> p t h c", t=T), 0, 0).then_inc(s_qkn, 1)
                st.do(by_rms(kn[:, :, :].rearrange("p t (h c) -> p t h c", c=HD), C, H))
                st.wait()
                v.tensor_tensor(kw[:, :, :].rearrange("p (t h) c -> p t (h c)", t=T), kn[:, :, :],
                                spread(qks[:, :].rearrange("p (a n) -> p a n", a=1), 1, T),
                                ALU.mult).then_inc(s_qkn, 1)

            def prep_low(b, st):
                dve.wait_ge(s_high, 2 * b + 1)
                q2 = spread(qn[:, :, :].rearrange("p n (a c) -> p n a c", a=1), 2, 2)
                k2 = spread(kw[:, :, :].rearrange("p n (a c) -> p n a c", a=1), 2, 2)
                q_hi, q_lo = stack[:, 0, :, 0, :, :], stack[:, 0, :, 1, :, :]
                k_hi, k_lo = stack[:, 1, :, :, 0, :], stack[:, 1, :, :, 1, :]
                st.do(v.tensor_tensor(q_lo, q2, q_hi, ALU.subtract))
                dve.wait_ge(s_high, 2 * b + 2)
                v.tensor_tensor(k_lo, k2, k_hi, ALU.subtract).then_inc(s_stack, 1)
                assert st.n == PREP_STEPS, st.n

            PREP_STEPS = (2 * T + 1) + (T - 1) + 2 * T + 4 + 3 * 3 + 3 + 1 + 1

            def o_norm(b, g, uses):
                dve.wait_ge(s_full, uses[f"oT{g}"] + 1)
                view = misc[:, :].rearrange("p (t j c) -> p t j c", t=T, c=32)
                v.reciprocal(recip[:, :, :], view[:, :, :, HD]).then_inc(s_attn, 1)
                dve.wait_ge(s_attn, b * G + g + 1)
                v.tensor_tensor(attn[:, :, 32 * g:32 * g + 32].rearrange("p t (j c) -> p t j c", c=HD),
                                view[:, :, :, 0:HD],
                                spread(recip[:, :, :].rearrange("p t (j a) -> p t j a", a=1), 3, HD),
                                ALU.mult).then_inc(s_free, 1)

            POST_STEPS = 2 * (2 * T + 1) + (T - 1) + 2
            TOP2_STEPS = 1 + T
            ROUTE_STEPS = TOP2_STEPS + 1 + T + 1 + 4 + 2 * T + 1

            def post_z(b, uses):
                st = Steps(dve, s_post, b, POST_STEPS)
                dve.wait_ge(s_full, uses["proj"] + 1)
                moments_of(st, lambda t: misc[:, t * C:(t + 1) * C], p_stats, p_moments, p_var, s_pvar)
                return st

            def post_x1(b, st):
                dve.wait_ge(s_prstd, 2 * b + 1)
                for t in range(T):
                    ins = v.scalar_tensor_tensor(out=tile_of(stream, b, t), in0=misc[:, t * C:(t + 1) * C],
                                                 scalar=p_rstd[:, t:t + 1], in1=tile_of(stream, b, t),
                                                 op0=ALU.mult, op1=ALU.add)
                    if t < T - 1:
                        st.do(ins)
                ins.then_inc(s_free, 1)

            def post_moments(b, st, uses):
                dve.wait_ge(s_free, uses["proj"] + 1)
                st.do(v.tensor_copy(held_dve[:, :], half[:, 0:1]))
                moments_of(st, lambda t: tile_of(stream, b, t), p_stats, p_moments, p_var, s_pvar, y_var)

            def post_v(b, st):
                for t in range(T):
                    ins = v.scalar_tensor_tensor(out=yv[:, t, :], in0=tile_of(stream, b, t),
                                                 scalar=p_moments[:, t, 0:1], in1=rms_sb[:, :],
                                                 op0=ALU.subtract, op1=ALU.mult)
                ins.then_inc(s_yv, 1)

            def post_y(b, st):
                dve.wait_ge(s_yhigh, b + 1)
                for t in range(T):
                    ins = v.scalar_tensor_tensor(out=y_split[:, 1, t, :], in0=yv[:, t, :],
                                                 scalar=y_rstd[:, t:t + 1], in1=y_split[:, 0, t, :],
                                                 op0=ALU.mult, op1=ALU.subtract)
                ins.then_inc(s_y, 1)
                assert st.n == POST_STEPS, st.n

            def top_2(b, uses):
                st = Steps(dve, s_route, b, ROUTE_STEPS)
                dve.wait_ge(s_full, uses["logits"] + 1)
                v.tensor_copy(logit[:, :, :], misc[:, 0:T * E].rearrange("p (t e) -> p t e", t=T)
                              ).then_inc(s_free, 1)
                dve.wait_ge(s_free, uses["logits"] + 1)
                st.do(v.tensor_copy(held_dve[:, :], half[:, 0:1]))
                for t in range(T):
                    st.do(v.max(top[:, t, :], logit[:, t, :]))
                st.wait()
                v.tensor_tensor(gap[:, :], top[:, :, 1], top[:, :, 0], ALU.subtract).then_inc(s_gap, 1)
                assert st.n == TOP2_STEPS

            def residual(b):
                dve.wait_ge(s_prstd, 2 * b + 2)
                for t in range(T):
                    v.tensor_scalar(xin[:, t, :], tile_of(stream, b, t), p_moments[:, t, 0:1],
                                    p_rstd[:, t:t + 1], ALU.subtract, ALU.mult)

            def router(b):
                st = Steps(dve, s_route, b, ROUTE_STEPS, TOP2_STEPS)
                st.do(v.tensor_copy(held_dve[:, :], half[:, 0:1]))
                for t in range(T):
                    st.do(v.max_index(top_at[:, t, :], top[:, t, :], logit[:, t, :]))
                st.wait()
                st.do(v.tensor_copy(top_no[:, :, :], top_at[:, :, 0:2]))
                dve.wait_ge(s_e2, b + 1)
                st.do(v.tensor_scalar(e_sum[:, :], e2[:, :], 1.0, None, ALU.add))
                st.wait()
                st.do(v.reciprocal(e_inv[:, :], e_sum[:, :]))
                st.wait()
                st.do(v.tensor_scalar(w_top[:, 0, :], e_inv[:, :], 0.5, None, ALU.mult))
                st.wait()
                st.do(v.tensor_tensor(w_top[:, 1, :], w_top[:, 0, :], e2[:, :], ALU.mult))
                st.wait()
                for n, dst in enumerate((w_a, w_b)):
                    for t in range(T):
                        st.do(v.tensor_scalar(dst[:, t, :], expert_no[:, :], top_no[:, t, n:n + 1],
                                              w_top[:, n, t:t + 1], ALU.is_equal, ALU.mult))
                st.wait()
                st.do(v.tensor_tensor(route[:, :], w_a[:, :, :].rearrange("p t e -> p (t e)"),
                                      w_b[:, :, :].rearrange("p t e -> p (t e)"), ALU.add))
                assert st.n == ROUTE_STEPS, st.n

            def hidden(b, k, banks, att):
                rows = PARTS[k % len(PARTS)][1]
                dve.wait_ge(s_tanh, b * TILES + k + 1)
                dve.wait_ge(s_hid, upto(b * TILES + k - 1))
                v.scalar_tensor_tensor(out=act2[0:rows, k % 2, :], in0=th[0:rows, k % 2, :], scalar=1.0,
                                       in1=up_banks[k % 2][0:rows, :], op0=ALU.add,
                                       op1=ALU.mult).then_inc(s_act, 1)
                dve.wait_ge(s_act, upto(b * TILES + k + 1))
                dve.wait_ge(s_gate, b * TILES + k + 1)
                dve.wait_ge(s_lo, upto(b * TILES + k + 1 - HR))
                v.tensor_tensor(hid[0:rows, k % HR, :], act2[0:rows, k % 2, :],
                                banks[k % len(banks)][0:rows, :], ALU.mult).then_inc(s_hid, 1)
                if high_on_dve(k, att):
                    dve.wait_ge(s_hid, upto(b * TILES + k + 1))
                    dve.wait_ge(s_dn, upto(b * TILES + k + 1 - HR))
                    v.tensor_copy(hid_hi[0:rows, k % HR, :], hid[0:rows, k % HR, :]).then_inc(s_hi_dve, 1)

            def combine(b, e, banks, acc):
                dve.wait_ge(s_dn, upto(b * TILES + (e + 1) * len(PARTS)))
                if e == 0:
                    dve.wait_ge(s_route, (b + 1) * ROUTE_STEPS)
                    if acc is not acc_last:
                        dve.wait_ge(s_result, upto(b))
                else:
                    dve.wait_ge(s_comb, upto(b * E + e))
                for t in range(T):
                    before = xin if e == 0 else acc
                    ins = v.scalar_tensor_tensor(out=acc[:, t, :],
                                                 in0=banks[e % len(banks)][:, t * C:(t + 1) * C],
                                                 scalar=route[:, t * E + e:t * E + e + 1],
                                                 in1=before[:, t, :], op0=ALU.mult, op1=ALU.add)
                ins.then_inc(s_comb, 1)

            FIN_STEPS = 3 * T + 1

            def final(b, acc):
                dve.wait_ge(s_comb, upto((b + 1) * E))
                st = Steps(dve, s_fin, b, FIN_STEPS)
                moments_of(st, lambda t: acc[:, t, :], f_stats, f_moments, f_var, s_fvar)

            def final_add(b, acc):
                st = Steps(dve, s_fin, b, FIN_STEPS, 2 * T + 1)
                dve.wait_ge(s_frstd, b + 1)
                normalised(st, lambda t: fn[:, t, :], lambda t: acc[:, t, :], f_moments, f_rstd)
                dve.wait_ge(s_out, upto(16 * b))
                st.wait()
                for t in range(T):
                    ins = v.tensor_tensor(result[:, t, :], fn[:, t, :], tile_of(stream, b, t), ALU.add)
                ins.then_inc(s_result, 1)
                assert st.n == FIN_STEPS

            def start():
                dve.wait_ge(s_const, 5)
                st = prep_ln(0)
                constants()
                prep_xn(0, st)
                prep_squares(0, st, Uses(None, True))
                prep_guess(0, st)
                for n in range(3):
                    prep_root(0, st, n)
                prep_inv(0, st)
                prep_norm(0, st)
                prep_low(0, st)
                for t in START_DVE:
                    name = f"stack{t}"
                    dve.wait_ge(s_qkt_full, t + 1)
                    v.tensor_copy(qkT[:, :, t * P:(t + 1) * P],
                                  misc_bank(name, None)[:, :].bitcast(F16).rearrange("p (a n) -> p a n", n=P)
                                  ).then_inc(s_qkt_free, 1)

            st_prep = st_post = None

            def run(att, ffn, prep, end, slots):
                nonlocal st_prep, st_post
                uses = uses_of(att, prep)
                g_banks, d_banks = gate_banks(att), down_banks(att)
                for s in slots:
                    if ffn is not None and s == TOP2:
                        top_2(ffn, uses)
                    if ffn is not None and s == RESIDUAL:
                        residual(ffn)
                    if ffn is not None and s == ROUTE:
                        router(ffn)
                    if att is not None and s in GROUP_NORM:
                        o_norm(att, GROUP_NORM[s], uses)
                    if ffn is not None:
                        hidden(ffn, s, g_banks, att)
                    if att is not None and s == POST_Y:
                        post_y(att, st_post)
                    if ffn is not None:
                        if s > LAG and (s - LAG + 1) % len(PARTS) == 0:
                            combine(ffn, (s - LAG + 1) // len(PARTS) - 1, d_banks,
                                    acc if att is not None else acc_last)
                    elif s in SPLIT:
                        split_weights(SPLIT.index(s))
                        if s == SPLIT[0]:
                            centre_projection()
                    if end is not None and s == final_slots(att)[1]:
                        combine(end, E - 1, down_banks(0), acc)
                    if end is not None and s == final_slots(att)[2]:
                        final(end, acc)
                    if end is not None and s == final_slots(att)[3]:
                        final_add(end, acc)
                    if prep is not None:
                        if s == PREP_LN:
                            st_prep = prep_ln(prep)
                        elif s == PREP_XN:
                            prep_xn(prep, st_prep)
                        elif s == PREP_SQUARES:
                            prep_squares(prep, st_prep, uses)
                        elif s == PREP_GUESS:
                            prep_guess(prep, st_prep)
                            prep_root(prep, st_prep, 0)
                        elif s == PREP_ROOT:
                            prep_root(prep, st_prep, 1)
                            prep_root(prep, st_prep, 2)
                        elif s == PREP_INV:
                            prep_inv(prep, st_prep)
                        elif s == PREP_NORM:
                            prep_norm(prep, st_prep)
                        elif s == PREP_LOW:
                            prep_low(prep, st_prep)
                    if att is not None:
                        if s == POST_Z:
                            st_post = post_z(att, uses)
                        elif s == POST_X1:
                            post_x1(att, st_post)
                        elif s == POST_MOMENTS:
                            post_moments(att, st_post, uses)
                        elif s == POST_V:
                            post_v(att, st_post)

            iterations(start, run, dve)
            combine(B - 1, E - 1, down_banks(None), acc_last)
            final(B - 1, acc_last)
            final_add(B - 1, acc_last)


def kernel(L0_attn_x, L0_attn_Wqkv, L0_attn_Wproj, L0_attn_bproj, L0_attn_q_scale, L0_attn_k_scale,
           L0_ffn_gate_w, L0_ffn_rms_w, L0_ffn_W1, L0_ffn_W2, L0_ffn_W3):
    import numpy as np
    import concourse.bacc as bacc
    from concourse.bass_utils import run_bass_kernel_spmd

    def rows(a, repeat=1):
        return np.ascontiguousarray(np.broadcast_to(np.tile(np.asarray(a), repeat), (P, a.shape[0] * repeat)))

    arrays = {
        "x": np.ascontiguousarray(L0_attn_x),
        "wqkv": np.ascontiguousarray(L0_attn_Wqkv),
        "wproj": np.ascontiguousarray(L0_attn_Wproj),
        "bproj": rows(L0_attn_bproj),
        "q_scale": rows(L0_attn_q_scale, H),
        "k_scale": rows(L0_attn_k_scale, H),
        "gate_wT": np.ascontiguousarray(np.asarray(L0_ffn_gate_w).T),
        "rms_w": rows(L0_ffn_rms_w),
        "w1T": np.ascontiguousarray(np.asarray(L0_ffn_W1).reshape(E * DE, C).T),
        "w2T": np.ascontiguousarray(np.asarray(L0_ffn_W2).reshape(E * DE, C).T),
        "w3T": np.ascontiguousarray(np.asarray(L0_ffn_W3).transpose(0, 2, 1)),
    }
    nc = bacc.Bacc("TRN2", target_bir_lowering=False, num_devices=1)
    args = [nc.dram_tensor(f"in_{name}", a.shape, mybir.dt.from_np(a.dtype), kind="ExternalInput").ap()
            for name, a in arrays.items()]
    out = nc.dram_tensor("out_dram", (B, N, C), F32, kind="ExternalOutput").ap()
    layers(nc, *args, out)
    r = run_bass_kernel_spmd(nc, [{f"in_{name}": a for name, a in arrays.items()}], core_ids=[0])
    return r.results[0]["out_dram"]
```
